# Optimizing a Trainium2 kernel written in Bass

```python
import numpy as np
import jax
import jax.numpy as jnp

def _softmax(x, axis=-1):
    return jax.nn.softmax(x, axis=axis)

def _gelu(x):
    return jax.nn.gelu(x, approximate=True)

def _silu(x):
    return jax.nn.silu(x)

def _sigmoid(x):
    return jax.nn.sigmoid(x)

def _layernorm(x, axis=-1, eps=1e-05):
    m = jnp.mean(x, axis=axis, keepdims=True)
    v = jnp.var(x, axis=axis, keepdims=True)
    return (x - m) / jnp.sqrt(v + eps)

def _scatter_add(tgt, idx, src, axis=0):
    return tgt.at[idx].add(src)

def _segment_sum(src, seg, n):
    return jax.ops.segment_sum(src, seg, n)
kernel_name = 'mk_flamingo_gated_d1_seqx_r8_53bad9'

def setup_inputs(seed: int=0):
    np.random.seed(seed)
    _w = jnp.asarray

    def _rec_inputs():
        import jax
        import jax.numpy as jnp
        _rk = jax.random.key(seed)
        x = 7.22e-05 + 1 * jax.random.normal(jax.random.fold_in(_rk, 1), (8, 128, 512), jnp.float32)
        _lenS = 128 - jax.random.randint(jax.random.fold_in(_rk, 7), (8,), 0, max(1, 128 // 4) + 1, jnp.int32)
        _lenS2 = 128 - jax.random.randint(jax.random.fold_in(_rk, 8), (8,), 0, max(1, 128 // 4) + 1, jnp.int32)
        _ctx_4096P = jax.random.normal(jax.random.fold_in(_rk, 11), (8, 16, 512), jnp.float32)
        _ctx_4096c = jax.random.dirichlet(jax.random.fold_in(_rk, 511), 0.3 * jnp.ones((16,), jnp.float32), (8, 128))
        _ctx_4096t = jnp.einsum('bsk,bkd->bsd', _ctx_4096c, _ctx_4096P)
        _ctx_4096t = _ctx_4096t * jax.lax.rsqrt(jnp.mean(jnp.square(_ctx_4096t)) + 1e-12) * 0.953939
        ctx_4096 = 4.13588e-05 + 0.999923 * (_ctx_4096t + 0.3 * jax.random.normal(jax.random.fold_in(_rk, 611), (8, 128, 512), jnp.float32))
        _validS = jnp.arange(128)[None, :] < _lenS[:, None]
        _validS2 = jnp.arange(128)[None, :] < _lenS2[:, None]
        _causal = jnp.tril(jnp.ones((128, 128), dtype=bool))
        mask_BxSxS2_bk0 = jnp.logical_not(jnp.broadcast_to(_validS2[:, None, :], (8, 128, 128)))
        _g = jax.random.normal(jax.random.fold_in(_rk, 9001), (2, 1), jnp.float32)
        _g = jnp.sign(_g) * jnp.maximum(jnp.abs(_g), 1.0) + (_g == 0) * 1.0
        g_xattn = _g[0]
        g_ffn = _g[1]
        return (x, ctx_4096, mask_BxSxS2_bk0, g_xattn, g_ffn)
    x, ctx_4096, mask_BxSxS2_bk0, g_xattn, g_ffn = _rec_inputs()

    def _L0_xattn_setup():
        import jax, jax.numpy as jnp
        import numpy as np
        B, LQ, LK, D, H, DH = (2, 128, 128, 512, 32, 128)
        EPS = 1e-05

        def _rmsnorm(x, weight):
            var = jnp.mean(jnp.square(x), axis=-1, keepdims=True)
            return x * jax.lax.rsqrt(var + EPS) * weight
        key = jax.random.key(seed)
        ks = jax.random.split(key, 8)
        scale = 0.02
        return {'hidden_states': jax.random.normal(ks[0], (B, LQ, D), jnp.float32), 'key_value_states': jax.random.normal(ks[1], (B, LK, D), jnp.float32), 'attention_mask': jax.random.randint(ks[2], (B, LQ, LK), 0, 2) > 0, 'position_bias': jax.random.normal(ks[3], (H, LQ, LK), jnp.float32), 'ln_weight': jnp.ones((D,), jnp.float32), 'w_q': jax.random.normal(ks[4], (H * DH, D), jnp.float32) * scale, 'w_k': jax.random.normal(ks[5], (H * DH, D), jnp.float32) * scale, 'w_v': jax.random.normal(ks[6], (H * DH, D), jnp.float32) * scale, 'w_out': jax.random.normal(ks[7], (D, H * DH), jnp.float32) * scale}
    _L0_xattn_all = _L0_xattn_setup()
    _L0_xattn_in = {k: v for k, v in _L0_xattn_all.items() if k in ('position_bias', 'ln_weight', 'w_q', 'w_k', 'w_v', 'w_out')}
    del _L0_xattn_all

    def _L0_ffn_setup():
        import jax, jax.numpy as jnp
        import numpy as np
        B_, S, D_IN, D_OUT = (4, 256, 512, 512)
        N, RANK, ALPHA = (8, 16, 32)
        SCALE = ALPHA / RANK
        key = jax.random.key(seed)
        kx, ka, kb, kw, kbias = jax.random.split(key, 5)
        x = jax.random.normal(kx, (B_, S, D_IN), dtype=jnp.float32)
        lora_A = jax.random.normal(ka, (N, RANK, D_IN), dtype=jnp.float32) * (1.0 / np.sqrt(D_IN))
        lora_B = jax.random.normal(kb, (N, D_OUT, RANK), dtype=jnp.float32) * (1.0 / np.sqrt(RANK))
        W = jax.random.normal(kw, (D_OUT, D_IN), dtype=jnp.float32) * (1.0 / np.sqrt(D_IN))
        bias = jax.random.normal(kbias, (D_OUT,), dtype=jnp.float32) * 0.01
        lora_weights = jnp.full((N,), 1.0 / N, dtype=jnp.float32)
        return {'x': x, 'lora_A': lora_A, 'lora_B': lora_B, 'W': W, 'bias': bias, 'lora_weights': lora_weights}
    _L0_ffn_all = _L0_ffn_setup()
    _L0_ffn_in = {k: v for k, v in _L0_ffn_all.items() if k in ('lora_A', 'lora_B', 'W', 'bias', 'lora_weights')}
    del _L0_ffn_all
    return {'x': x, 'ctx_4096': ctx_4096, 'mask_BxSxS2_bk0': mask_BxSxS2_bk0, 'g_xattn': g_xattn, 'g_ffn': g_ffn, 'L0_xattn_position_bias': _L0_xattn_in['position_bias'], 'L0_xattn_ln_weight': _L0_xattn_in['ln_weight'], 'L0_xattn_w_q': _L0_xattn_in['w_q'], 'L0_xattn_w_k': _L0_xattn_in['w_k'], 'L0_xattn_w_v': _L0_xattn_in['w_v'], 'L0_xattn_w_out': _L0_xattn_in['w_out'], 'L0_ffn_lora_A': _L0_ffn_in['lora_A'], 'L0_ffn_lora_B': _L0_ffn_in['lora_B'], 'L0_ffn_W': _L0_ffn_in['W'], 'L0_ffn_bias': _L0_ffn_in['bias'], 'L0_ffn_lora_weights': _L0_ffn_in['lora_weights']}

def reference(x, ctx_4096, mask_BxSxS2_bk0, g_xattn, g_ffn, L0_xattn_position_bias, L0_xattn_ln_weight, L0_xattn_w_q, L0_xattn_w_k, L0_xattn_w_v, L0_xattn_w_out, L0_ffn_lora_A, L0_ffn_lora_B, L0_ffn_W, L0_ffn_bias, L0_ffn_lora_weights):
    import jax
    import jax.numpy as jnp

    def _L0_xattn_ref(hidden_states, key_value_states, attention_mask, position_bias, ln_weight, w_q, w_k, w_v, w_out):
        import jax, jax.numpy as jnp
        import numpy as np
        B, LQ, LK, D, H, DH = (2, 128, 128, 512, 32, 128)
        EPS = 1e-05

        def _rmsnorm(x, weight):
            var = jnp.mean(jnp.square(x), axis=-1, keepdims=True)
            return x * jax.lax.rsqrt(var + EPS) * weight
        x = _rmsnorm(hidden_states, ln_weight)
        b, lq, _ = x.shape
        lk = key_value_states.shape[1]
        h_q = (x @ w_q.T).reshape(b, lq, H, DH)
        h_k = (key_value_states @ w_k.T).reshape(b, lk, H, DH)
        h_v = (key_value_states @ w_v.T).reshape(b, lk, H, DH)
        score = jnp.einsum('bqhd,bkhd->bhqk', h_q, h_k)
        score = score + position_bias[None]
        m = attention_mask[:, None]
        score = jnp.where(m, score, -jnp.inf)
        score = jax.nn.softmax(score, axis=-1)
        score = jnp.where(m, score, 0.0)
        attn = jnp.einsum('bhqk,bkhd->bqhd', score, h_v).reshape(b, lq, H * DH)
        out = attn @ w_out.T
        return hidden_states + out

    def _L0_ffn_ref(x, lora_A, lora_B, W, bias, lora_weights):
        import jax, jax.numpy as jnp
        import numpy as np
        B_, S, D_IN, D_OUT = (4, 256, 512, 512)
        N, RANK, ALPHA = (8, 16, 32)
        SCALE = ALPHA / RANK
        h = jnp.einsum('bsd,nrd->nbsr', x, lora_A)
        coef = (SCALE * lora_weights)[:, None, None]
        lora_out = jnp.einsum('nbsr,nor->bso', h, lora_B * coef)
        base = jnp.einsum('bsd,od->bso', x, W) + bias
        return base + lora_out
    x = x + jnp.tanh(g_xattn[0]) * _L0_xattn_ref(_layernorm(x, axis=-1), ctx_4096, mask_BxSxS2_bk0, L0_xattn_position_bias, L0_xattn_ln_weight, L0_xattn_w_q, L0_xattn_w_k, L0_xattn_w_v, L0_xattn_w_out)
    x = x + jnp.tanh(g_ffn[0]) * _L0_ffn_ref(_layernorm(x, axis=-1), L0_ffn_lora_A, L0_ffn_lora_B, L0_ffn_W, L0_ffn_bias, L0_ffn_lora_weights)
    return x

_drawn_inputs = setup_inputs


def setup_inputs(seed=0):
    import zlib

    import numpy as np

    out = dict(_drawn_inputs(seed))
    spreads = {'L0_xattn_ln_weight': (1.0, 0.554), 'L0_ffn_lora_weights': (0.125, 0.2)}
    factors = {'L0_ffn_bias': 8.0}
    for name, (base, spread) in spreads.items():
        noise = np.random.default_rng([zlib.crc32(name.encode()), seed]).standard_normal(out[name].shape)
        drawn = base * np.exp(spread * noise) if base else spread * noise
        out[name] = jnp.asarray(drawn.astype(out[name].dtype))
    for name, factor in factors.items():
        out[name] = (out[name] * factor).astype(out[name].dtype)
    return out
```

```python
import concourse.bass as bass
from concourse import mybir
from contextlib import ExitStack

FP32 = mybir.dt.float32
FP32R = mybir.dt.float32r
U8 = mybir.dt.uint8
ALU = mybir.AluOpType
ACT = mybir.ActivationFunctionType
AX = mybir.AxisListType

B, S, D = 8, 128, 512
H, DH = 32, 128
P = 128
NC = D // P
HB = B // 2
HT = HB * S
PAIRS = H // 2
N_LORA, RANK = 8, 16
EPS = 1e-5
SQ = 32
NSQ = S // SQ
LORA_SCALE = 2.0
MASKED = 1e30


def gated_block(nc, x, ctx_t, mask, g_xattn, g_ffn, bias, ln_w, wq, wk, wv, wo,
                lora_a, lora_bt, w_t, ffn_bias, lora_w, out):
    stack = ExitStack()
    with stack:
        def sb(name, shape, dt=FP32):
            return stack.enter_context(nc.sbuf_tensor(name, shape, dt))

        def ps(name):
            return stack.enter_context(nc.psum_tensor(name, [P, 512], FP32))

        def sem(name):
            return stack.enter_context(nc.semaphore(name))

        x_tok = sb("x_tok", [P, B, D])
        acc = sb("acc", [P, B, D])
        xn_hi = sb("xn_hi", [P, NC, B * S], FP32R)
        xn_lo = sb("xn_lo", [P, NC, B * S], FP32R)
        cx_hi = sb("cx_hi", [P, NC, B * S], FP32R)
        cx_lo = sb("cx_lo", [P, NC, B * S], FP32R)
        wqk_stage = sb("wqk_stage", [P, 2, 2, D])
        wqk_hi = sb("wqk_hi", [P, 2, 2, D], FP32R)
        wqk_lo = sb("wqk_lo", [P, 2, 2, D], FP32R)
        wv_stage = sb("wv_stage", [P, NC, 2 * DH])
        wv_hi = sb("wv_hi", [P, NC, 2 * DH], FP32R)
        wv_lo = sb("wv_lo", [P, NC, 2 * DH], FP32R)
        wo_stage = sb("wo_stage", [P, 2, D])
        wo_hi = sb("wo_hi", [P, 2, D], FP32R)
        wo_lo = sb("wo_lo", [P, 2, D], FP32R)
        q_t = sb("q_t", [P, HT])
        k_t = sb("k_t", [P, HT])
        v_tok = sb("v_tok", [P, 2, HB, 2 * DH])
        at_hi = sb("at_hi", [P, 2, HT], FP32R)
        at_lo = sb("at_lo", [P, 2, HT], FP32R)
        scores = sb("scores", [P, HT])
        prob = sb("prob", [P, HT])
        prob_t = sb("prob_t", [P, HT])
        prob_dram = nc.dram_tensor("prob_scratch", (2, P, HT), FP32).ap()
        bias_stage = sb("bias_stage", [P, 2, S])
        bias_mask = sb("bias_mask", [P, 2, HB, S])
        mask_u8 = sb("mask_u8", [P, B, S], U8)
        mask_add = sb("mask_add", [P, B, S])
        row_used = sb("row_used", [P, B])
        row_best = sb("row_best", [P, B])
        neg_max_t = sb("neg_max_t", [P, HB])
        row_sum = sb("row_sum", [P, HB])
        row_inv = sb("row_inv", [P, HB])
        ident = sb("ident", [P, P])
        neg_half = sb("neg_half", [P, 2, HB])
        ln_w_b = sb("ln_w_b", [P, D])
        ffn_bias_b = sb("ffn_bias_b", [P, D])
        bn = sb("bn", [P, B, 6])
        mean_var = sb("mean_var", [P, B, 2])
        norm_in = sb("norm_in", [P, 2, B])
        norm_out = sb("norm_out", [P, 2, B])
        norm_v = sb("norm_v", [P, 2, B])
        gate_in = sb("gate_in", [P, 2])
        gate = sb("gate", [P, 2])
        lora_w_col = sb("lora_w_col", [P, 1])
        lora_a_sb = sb("lora_a_sb", [P, D])
        lora_b_sb = sb("lora_b_sb", [P, D])
        wf_hi = sb("wf_hi", [P, NC, D], FP32R)
        wf_lo = sb("wf_lo", [P, NC, D], FP32R)
        wf = wqk_stage[:, :, :, :].rearrange("p a b n -> p (a b) n")
        scores_b, prob_b = (t[:, :].rearrange("p (b n) -> p b n", b=HB) for t in (scores, prob))
        ve, rms_in, rstd, rms = norm_in[:, 0, :], norm_in[:, 1, :], norm_out[:, 0, :], norm_out[:, 1, :]
        ve_inv, neg_mean = norm_v[:, 0, :], norm_v[:, 1, :]

        ps_s, ps_q, ps_k, ps_t, ps_pv, ps_z = (ps(n) for n in ("ps_s", "ps_q", "ps_k", "ps_t", "ps_pv", "ps_z"))
        ps_x = [ps("ps_x0"), ps("ps_x1")]
        ps_f = [ps_q, ps_k]

        x_in = [sem(f"x_in{t}") for t in range(B)]
        cx_first_in = [sem(f"cx_first_in{c}") for c in range(NC)]
        cx_second_in, first_k_in = sem("cx_second_in"), sem("first_k_in")
        wqk_in = [sem(f"wqk_in{j}") for j in range(2)]
        wv_in, wo_in, bias_in, mask_in = sem("wv_in"), sem("wo_in"), sem("bias_in"), sem("mask_in")
        gate_ld, ln_w_in, lora_in, wf_in = sem("gate_ld"), sem("ln_w_in"), sem("lora_in"), sem("wf_in")
        out_stored = sem("out_stored")
        cx_hi_done, cx_first_split, cx_second_split = sem("cx_hi_done"), sem("cx_first_split"), sem("cx_second_split")
        first_k_hi, first_k_split, first_v_rest = sem("first_k_hi"), sem("first_k_split"), sem("first_v_rest")
        wqk_hi_done = [sem(f"wqk_hi_done{j}") for j in range(2)]
        wqk_split = [sem(f"wqk_split{j}") for j in range(2)]
        wv_hi_done, wv_split, wo_hi_done, wo_split = (sem(n) for n in ("wv_hi_done", "wv_split", "wo_hi_done", "wo_split"))
        consts = sem("consts")
        norm_in_ready, norm_out_ready = sem("norm_in_ready"), sem("norm_out_ready")
        rstd_ready, y_done, xs_done = (sem(n) for n in ("rstd_ready", "y_done", "xs_done"))
        z_turned, z_hi_done, z_split = sem("z_turned"), sem("z_hi_done"), sem("z_split")
        pool_step, vec_step = sem("pool_step"), sem("vec_step")
        q_done, q_copied, k_done, k_copied = (sem(n) for n in ("q_done", "q_copied", "k_done", "k_copied"))
        s_done, bm_ready, s_biased, neg_max, exp_done, row_inv_done, row_scale, p_norm, p_turned, p_sent = (
            sem(n) for n in ("s_done", "bm_ready", "s_biased", "neg_max", "exp_done", "row_inv_done", "row_scale", "p_norm", "p_turned", "p_sent"))
        pt_in, pv_done, at_hi_done, at_split = (sem(n) for n in ("pt_in", "pv_done", "at_hi_done", "at_split"))
        v_done, v_copied = sem("v_done"), sem("v_copied")
        o_done, o_added = sem("o_done"), sem("o_added")
        gate_ready, mask_ready, used_ready = sem("gate_ready"), sem("mask_ready"), sem("used_ready")
        lora_scaled, m_done, m_added, m_hi_done, m_split = (sem(n) for n in ("lora_scaled", "m_done", "m_added", "m_hi_done", "m_split"))
        x_gated = sem("x_gated")
        bias_gated, x2_done, z_normed, x2_biased, f_done, f_out = (
            sem(n) for n in ("bias_gated", "x2_done", "z_normed", "x2_biased", "f_done", "f_out"))

        block = stack.enter_context(nc.Block())

        def as_f32(ap):
            return ap.bitcast(FP32)

        ctx_stage = [v_tok[:, :, :, :].rearrange("p s b n -> p (s b n)").rearrange("p (c n) -> p c n", c=NC),
                     acc[:, HB:B, :]]
        xs = [lora_a_sb[:, :], lora_b_sb[:, :], scores[:, :], prob[:, :]] + [lora_a_sb[:, :], lora_b_sb[:, :]] * 2

        def turned(n):
            if n < HB:
                return (ps_z, ps_pv, ps_s, ps_t)[n]
            return ps_z if n % 2 == 0 else ps_t

        def tokens(t):
            return slice(t * S, (t + 1) * S)

        def half(s):
            return slice(s * HT, (s + 1) * HT)

        @block.sync
        def _(sp):
            def load_wqk(p, j):
                sp.dma_start(wqk_stage[:, j, 0, :], wq[2 * p + j]).then_inc(wqk_in[j], 16)
                sp.dma_start(wqk_stage[:, j, 1, :], wk[2 * p + j]).then_inc(wqk_in[j], 16)

            sp.dma_start(ctx_stage[0][:, 0, :], ctx_t[0, :, 0, :]).then_inc(cx_first_in[0], 16)
            sp.dma_start(wqk_stage[:, 0, 1, :], wk[0]).then_inc(first_k_in, 16)
            for c in range(1, NC):
                sp.dma_start(ctx_stage[0][:, c, :], ctx_t[0, :, c, :]).then_inc(cx_first_in[c], 16)
            sp.dma_start(wv_stage[:, :, :], wv[0]).then_inc(wv_in, 16)
            for t in range(HB):
                sp.dma_start(x_tok[:, t, :], x[t]).then_inc(x_in[t], 16)
            load_wqk(0, 1)
            sp.dma_start(ln_w_b[:, :], ln_w.partition_broadcast(P)).then_inc(ln_w_in, 16)
            sp.dma_start(wqk_stage[:, 0, 0, :], wq[0]).then_inc(wqk_in[0], 16)
            for t in range(HB, B):
                sp.dma_start(x_tok[:, t, :], x[t]).then_inc(x_in[t], 16)
            sp.dma_start(mask_u8[:, :, :], mask).then_inc(mask_in, 16)
            sp.dma_start(bias_stage[:, :, :], bias[0]).then_inc(bias_in, 16)
            sp.dma_start(ctx_stage[1], ctx_t[1]).then_inc(cx_second_in, 16)
            sp.dma_start(wo_stage[:, :, :], wo[0]).then_inc(wo_in, 16)
            sp.dma_start(gate_in[:, 0:1], g_xattn.partition_broadcast(P)).then_inc(gate_ld, 16)
            sp.dma_start(gate_in[:, 1:2], g_ffn.partition_broadcast(P)).then_inc(gate_ld, 16)
            sp.dma_start(ffn_bias_b[:, :], ffn_bias.partition_broadcast(P)).then_inc(gate_ld, 16)

            def move_probs(p, k):
                u = 4 * p + k
                sp.wait_ge(p_turned, u + 1)
                sp.dma_start(prob_dram[k % 2], prob[:, :]).then_inc(p_sent, 16)
                sp.wait_ge(p_sent, 16 * (u + 1))
                if not (isinstance(u, int) and u == 0):
                    sp.wait_ge(pv_done, u)
                for j in range(NSQ):
                    sp.dma_start(prob_t[j * SQ:(j + 1) * SQ, :].rearrange("a (i r) -> a i r", i=NSQ),
                                 prob_dram[k % 2, :, j * P:(j + 1) * P].rearrange("(i a) r -> a i r", a=SQ)).then_inc(pt_in, 16)

            def prefetch(p, k):
                if k == 0:
                    sp.wait_ge(wqk_split[0], p + 1)
                    load_wqk(p + 1, 0)
                if k == 1:
                    sp.wait_ge(wqk_split[1], p + 1)
                    load_wqk(p + 1, 1)
                    sp.wait_ge(wv_split, p + 1)
                    sp.dma_start(wv_stage[:, :, :], wv[p + 1]).then_inc(wv_in, 16)
                if k == 2:
                    sp.wait_ge(bm_ready, 4 * p + 4)
                    sp.dma_start(bias_stage[:, :, :], bias[p + 1]).then_inc(bias_in, 16)
                if k == 3:
                    sp.wait_ge(wo_split, p + 1)
                    sp.dma_start(wo_stage[:, :, :], wo[p + 1]).then_inc(wo_in, 16)

            sp.wait_ge(first_v_rest, 1)
            for k in range(4):
                move_probs(0, k)
                prefetch(0, k)
            sp.wait_ge(z_turned, B)
            sp.dma_start(lora_a_sb[:, :], lora_a).then_inc(lora_in, 16)
            sp.dma_start(lora_b_sb[:, :], lora_bt).then_inc(lora_in, 16)
            sp.dma_start(lora_w_col[:, :], lora_w).then_inc(lora_in, 16)
            with sp.Fori(1, PAIRS - 1) as p:
                for k in range(4):
                    move_probs(p, k)
                    prefetch(p, k)
            for j in range(2):
                sp.wait_ge(wqk_split[j], PAIRS)
            sp.dma_start(wf, w_t).then_inc(wf_in, 16)
            for k in range(4):
                move_probs(PAIRS - 1, k)
            for t in range(B):
                sp.wait_ge(f_out, t + 1)
                sp.dma_start(out[t], acc[:, t, :]).then_inc(out_stored, 16)
            sp.wait_ge(out_stored, 16 * B)

        @block.gpsimd
        def _(pool):
            step = [0]

            def link(ins):
                step[0] += 1
                ins.then_inc(pool_step, 1)
                pool.wait_ge(pool_step, step[0])

            g = nc.gpsimd
            link(g.memset(ident[:, :], 0.0))
            link(g.affine_select(out=ident[:, :], in_=ident[:, :], compare_op=ALU.not_equal, fill=1.0,
                                 base=0, pattern=[[-1, P]], channel_multiplier=1))
            g.memset(neg_half[:, :, :], -0.5).then_inc(consts, 1)
            pool.wait_ge(consts, 1)

            def norm_scales(s):
                h = slice(s * HB, (s + 1) * HB)
                pool.wait_ge(norm_in_ready, s + 1)
                g.tensor_tensor(out=norm_out[:, :, h], in0=norm_in[:, :, h], in1=neg_half[:, :, :],
                                op=ALU.pow).then_inc(norm_out_ready, 1)

            def bias_and_mask(p, k):
                s, j = k // 2, k % 2
                if k == 0:
                    pool.wait_ge(bias_in, 16 * (p + 1))
                if not (isinstance(p, int) and 4 * p + k < 2):
                    pool.wait_ge(s_biased, 4 * p + k - 1)
                g.tensor_tensor(out=bias_mask[:, j, :, :],
                                in0=bias_stage[:, j, :].unsqueeze(1).to_broadcast([P, HB, S]),
                                in1=mask_add[:, s * HB:(s + 1) * HB, :], op=ALU.add).then_inc(bm_ready, 1)

            pool.wait_ge(wv_hi_done, 1)
            g.tensor_tensor(out=wv_lo[:, NC // 2:, :], in0=wv_stage[:, NC // 2:, :],
                            in1=as_f32(wv_hi[:, NC // 2:, :]), op=ALU.subtract).then_inc(first_v_rest, 1)
            norm_scales(0)
            pool.wait_ge(mask_in, 16)
            g.tensor_scalar(mask_add[:, :, :], mask_u8[:, :, :], MASKED, -MASKED, ALU.mult, ALU.add).then_inc(mask_ready, 1)
            pool.wait_ge(mask_ready, 1)
            bias_and_mask(0, 0)
            for c in range(NC):
                if c == NC // 2:
                    norm_scales(1)
                pool.wait_ge(cx_hi_done, NC + c + 1)
                g.tensor_tensor(out=cx_lo[:, c, half(1)], in0=ctx_stage[1][:, c, :],
                                in1=as_f32(cx_hi[:, c, half(1)]), op=ALU.subtract).then_inc(cx_second_split, 1)
            for k in range(1, 4):
                bias_and_mask(0, k)
            with pool.Fori(1, PAIRS - 1) as p:
                for k in range(4):
                    bias_and_mask(p, k)

            pool.wait_ge(lora_in, 48)
            g.tensor_scalar(lora_b_sb[:, :], lora_b_sb[:, :], lora_w_col[:, 0:1], LORA_SCALE,
                            ALU.mult, ALU.mult).then_inc(lora_scaled, 1)
            pool.wait_ge(gate_ready, 1)
            g.tensor_scalar(ffn_bias_b[:, :], ffn_bias_b[:, :], gate[:, 1:2], 1.0,
                            ALU.mult, ALU.mult).then_inc(bias_gated, 1)
            pool.wait_ge(bias_gated, 1)

            for k in range(4):
                bias_and_mask(PAIRS - 1, k)

            def x2_scale(t):
                pool.wait_ge(x2_done, t + 1)
                link(g.tensor_scalar(ve[:, t:t + 1], mean_var[:, t, 1:2], EPS, None, ALU.add))
                link(g.tensor_tensor(out=rstd[:, t:t + 1], in0=ve[:, t:t + 1], in1=neg_half[:, 0, 0:1], op=ALU.pow))
                g.tensor_scalar(neg_mean[:, t:t + 1], mean_var[:, t, 0:1], rstd[:, t:t + 1], -1.0,
                                ALU.mult, ALU.mult).then_inc(rstd_ready, 1)

            def x2_bias(t):
                pool.wait_ge(z_normed, t + 1)
                g.tensor_tensor(out=x_tok[:, t, :], in0=x_tok[:, t, :], in1=ffn_bias_b[:, :],
                                op=ALU.add).then_inc(x2_biased, 1)

            x2_scale(0)
            for t in range(1, B):
                x2_scale(t)
                x2_bias(t - 1)
            x2_bias(B - 1)

        @block.tensor
        def _(pe):
            def three(o, l_hi, l_lo, r_hi, r_lo, start, stop):
                nc.tensor.matmul(o, l_hi, r_hi, start=start, stop=False)
                nc.tensor.matmul(o, l_hi, r_lo, start=False, stop=False)
                return nc.tensor.matmul(o, l_lo, r_hi, start=False, stop=stop)

            def project(k, key, arriving=False):
                s, j = k // 2, k % 2
                o, r_hi, r_lo = (ps_k, cx_hi, cx_lo) if key else (ps_q, xn_hi, xn_lo)
                for c in range(NC):
                    if arriving:
                        pe.wait_ge(cx_first_split, c + 1)
                    w = slice(c * DH, (c + 1) * DH)
                    last = three(o[:, :], wqk_hi[:, j, int(key), w], wqk_lo[:, j, int(key), w],
                                 r_hi[:, c, half(s)], r_lo[:, c, half(s)], c == 0, c == NC - 1)
                last.then_inc(k_done if key else q_done, 1)

            def values(s, added=None):
                for i in range(2):
                    if added is not None:
                        pe.wait_ge(o_added, added + i)
                    for b in (2 * i, 2 * i + 1):
                        o = ps_x[i][:, (b % 2) * 2 * DH:(b % 2 + 1) * 2 * DH]
                        for c in range(NC):
                            last = three(o, cx_hi[:, c, tokens(s * HB + b)], cx_lo[:, c, tokens(s * HB + b)],
                                         wv_hi[:, c, :], wv_lo[:, c, :], c == 0, c == NC - 1)
                    last.then_inc(v_done, 1)

            def turn(src, n, ready):
                pe.wait_ge(ready, n % B + 1)
                if n >= HB:
                    pe.wait_ge(z_split, n - 1)
                for c in range(NC):
                    last = nc.tensor.transpose(turned(n)[:, c * P:(c + 1) * P], src[:, c * P:(c + 1) * P], ident[:, :])
                last.then_inc(z_turned, 1)

            def out_tile(first, b, wo_pair, units, copied=None):
                if b == 0:
                    pe.wait_ge(wo_split, wo_pair + 1)
                    pe.wait_ge(at_split, units)
                if b < 2 and copied is not None:
                    pe.wait_ge(v_copied, copied)
                else:
                    pe.wait_ge(o_added, first + b - 1)
                for j in range(2):
                    last = three(ps_x[b % 2][:, :], at_hi[:, j, tokens(b)], at_lo[:, j, tokens(b)],
                                 wo_hi[:, j, :], wo_lo[:, j, :], j == 0, j == 1)
                last.then_inc(o_done, 1)

            def score(p, k):
                u = 4 * p + k
                pe.wait_ge(q_copied, u + 1)
                pe.wait_ge(k_copied, u + 1)
                if not (isinstance(u, int) and u == 0):
                    pe.wait_ge(s_biased, u)
                for b in range(HB):
                    last = nc.tensor.matmul(ps_s[:, tokens(b)], q_t[:, tokens(b)], k_t[:, tokens(b)], start=True, stop=True)
                last.then_inc(s_done, 1)

            def attend(p, k):
                u, s, j = 4 * p + k, k % 4 // 2, k % 2
                pe.wait_ge(pt_in, 16 * NSQ * (u + 1))
                if j == 0:
                    pe.wait_ge(v_copied, u + 2)
                if not (isinstance(u, int) and u == 0):
                    pe.wait_ge(at_split, u)
                pt = prob_t[:, :].rearrange("p (i b r) -> p b i r", i=NSQ, b=HB)
                for b in range(HB):
                    last = nc.tensor.matmul(ps_pv[:, tokens(b)], v_tok[:, s, b, j * DH:(j + 1) * DH],
                                            pt[:, b, :, :], start=True, stop=True)
                last.then_inc(pv_done, 1)

            def unit(p, k, first=False, last=False):
                u = 4 * p + k
                out_from = None if k % 2 == 0 or (first and k == 1) else 8 * p - 6 + 2 * k
                score(p, k)
                if out_from is not None:
                    for b in range(2):
                        out_tile(out_from, b, p - (k == 1), u - 1, copied=u + 1)
                nk = (k + 1) % 4
                pe.wait_ge(wqk_split[nk % 2], p + 1 + (k == 3))
                if first and k == 1:
                    pe.wait_ge(z_split, B)
                    pe.wait_ge(cx_second_split, NC)
                project(nk, False)
                if not (first and k == 0):
                    project(nk, True)
                if out_from is not None:
                    for b in range(2, HB):
                        out_tile(out_from, b, p - (k == 1), u - 1)
                if not (first and k == 0):
                    attend(p, k - 1)
                if k % 2 == 0 and not (first and k == 0) and not (last and k == 2):
                    pe.wait_ge(wv_split, p + 1)
                    values(k // 2, added=None if first else 8 * p - 5 + 2 * k)
                if last:
                    for c in ((0, 1), (2,), (3,))[k]:
                        merge(c)

            def merge(c):
                if c == 0:
                    pe.wait_ge(lora_scaled, 1)
                else:
                    pe.wait_ge(m_added, c)
                nc.tensor.matmul(ps_z[:, :], lora_a_sb[:, c * P:(c + 1) * P], lora_b_sb[:, :],
                                 start=True, stop=True).then_inc(m_done, 1)

            def ffn(t):
                pe.wait_ge(z_split, B + t + 1)
                if t == 0:
                    pe.wait_ge(m_split, NC)
                if t >= 2:
                    pe.wait_ge(f_out, t - 1)
                for c in range(NC):
                    last = three(ps_f[t % 2][:, :], xn_hi[:, c, tokens(t)], xn_lo[:, c, tokens(t)],
                                 wf_hi[:, c, :], wf_lo[:, c, :], c == 0, c == NC - 1)
                last.then_inc(f_done, 1)

            pe.wait_ge(first_k_split, 1)
            project(0, True, arriving=True)
            pe.wait_ge(wv_split, 1)
            pe.wait_ge(first_v_rest, 1)
            values(0)
            pe.wait_ge(wqk_split[1], 1)
            pe.wait_ge(k_copied, 1)
            project(1, True)
            pe.wait_ge(consts, 1)
            for t in range(HB):
                turn(xs[t], t, xs_done)
            pe.wait_ge(wqk_split[0], 1)
            pe.wait_ge(z_split, HB)
            project(0, False)

            unit(0, 0, first=True)
            for t in range(HB, B):
                turn(xs[t], t, xs_done)
            for k in range(1, 4):
                unit(0, k, first=True)
            with pe.Fori(1, PAIRS - 1) as p:
                for k in range(4):
                    unit(p, k)
            p = PAIRS - 1
            for k in range(3):
                unit(p, k, last=True)

            def turn_z(t):
                turn(acc[:, t, :], B + t, z_normed)

            score(p, 3)
            for b in range(HB):
                out_tile(8 * p, b, p, 4 * p + 2)
            values(1, added=8 * p + 3)
            turn_z(0)
            turn_z(1)
            attend(p, 2)
            ffn(0)
            turn_z(2)
            attend(p, 3)
            ffn(1)
            turn_z(3)
            for b in range(HB):
                out_tile(8 * p + 4, b, p, 4 * p + 4, copied=4 * p + 4)
            for t in range(2, B):
                ffn(t)
                if t + 2 < B:
                    turn_z(t + 2)

        @block.scalar
        def _(act):
            a = nc.scalar

            def z_hi(n):
                act.wait_ge(z_turned, n + 1)
                a.copy(xn_hi[:, :, tokens(n % B)], turned(n)[:, :].rearrange("p (c n) -> p c n", c=NC)).then_inc(z_hi_done, 1)

            def copy_q(u):
                act.wait_ge(q_done, u + 1)
                if not (isinstance(u, int) and u == 0):
                    act.wait_ge(s_done, u)
                a.copy(q_t[:, :], ps_q[:, :]).then_inc(q_copied, 1)

            def copy_k(u):
                act.wait_ge(k_done, u + 1)
                if not (isinstance(u, int) and u == 0):
                    act.wait_ge(s_done, u)
                a.copy(k_t[:, :], ps_k[:, :]).then_inc(k_copied, 1)

            def copy_v_bank(blocks, s, i):
                act.wait_ge(v_done, 2 * blocks + i + 1)
                a.copy(v_tok[:, s, 2 * i:2 * i + 2, :].rearrange("p b n -> p (b n)"), ps_x[i][:, :]).then_inc(v_copied, 1)

            def copy_v(blocks, s):
                for i in range(2):
                    copy_v_bank(blocks, s, i)

            def attended_hi(u, j):
                act.wait_ge(pv_done, u + 1)
                a.copy(at_hi[:, j, :], ps_pv[:, :]).then_inc(at_hi_done, 1)

            def exps(u):
                act.wait_ge(neg_max, u + 1)
                if not (isinstance(u, int) and u == 0):
                    act.wait_ge(p_sent, 16 * u)
                for b in range(HB):
                    last = a.activation(prob[:, tokens(b)], scores[:, tokens(b)], ACT.Exp, bias=neg_max_t[:, b:b + 1],
                                        scale=1.0, accum_out=row_sum[:, b:b + 1])
                last.then_inc(exp_done, 1)

            def hi_wqk(n, j, used):
                act.wait_ge(wqk_in[j], 32 * n - 16 * (j == 0))
                if used is not None:
                    act.wait_ge(k_done, used)
                a.copy(wqk_hi[:, j, :, :], wqk_stage[:, j, :, :]).then_inc(wqk_hi_done[j], 1)

            def hi_wv(n, used):
                act.wait_ge(wv_in, 16 * n)
                if used is not None:
                    act.wait_ge(v_done, used)
                a.copy(wv_hi[:, :, :], wv_stage[:, :, :]).then_inc(wv_hi_done, 1)

            def hi_wo(n, used):
                act.wait_ge(wo_in, 16 * n)
                if used is not None:
                    act.wait_ge(o_done, used)
                a.copy(wo_hi[:, :, :], wo_stage[:, :, :]).then_inc(wo_hi_done, 1)

            def hi_cx(s, c):
                act.wait_ge(cx_second_in if s else cx_first_in[c], 16)
                a.copy(cx_hi[:, c, half(s)], ctx_stage[s][:, c, :]).then_inc(cx_hi_done, 1)

            def layer_norm(t):
                a.activation(acc[:, t, :], x_tok[:, t, :], ACT.Identity, bias=neg_mean[:, t:t + 1],
                             scale=rstd[:, t:t + 1]).then_inc(y_done, 1)

            def weights_hi(p, k, first):
                if k == 2:
                    hi_wo(p + 1, None if first else 8 * p)
                    hi_wqk(p + 2, 0, 4 * p + 3)
                if k == 3:
                    hi_wqk(p + 2, 1, 4 * p + 4)
                    hi_wv(p + 2, 4 * p + 4)

            def unit(p, k, first=False, last=False):
                u = 4 * p + k
                if k % 2 == 0 and not (first and k == 0):
                    attended_hi(u - 2, 0)
                exps(u)
                if first and k == 0:
                    act.wait_ge(rstd_ready, 2)
                    for t in range(HB, B):
                        second_norm(t)
                if last and k == 2:
                    hi_wo(p + 1, 8 * p)
                if not last:
                    weights_hi(p, k, first)
                copy_q(u + 1)
                copy_k(u + 1)
                if k % 2 == 0 and not (first and k == 0):
                    attended_hi(u - 1, 1)
                    if not (last and k == 2):
                        copy_v(2 * p + k // 2, k // 2)
                if last:
                    for c in ((0, 1), (2,), (3,))[k]:
                        merged_hi(c)

            def merged_hi(c):
                act.wait_ge(m_added, c + 1)
                a.copy(wf_hi[:, c, :], wf[:, c, :]).then_inc(m_hi_done, 1)

            hi_cx(0, 0)
            act.wait_ge(first_k_in, 16)
            a.copy(wqk_hi[:, 0, 1, :], wqk_stage[:, 0, 1, :]).then_inc(first_k_hi, 1)
            for c in range(1, NC):
                hi_cx(0, c)
            hi_wv(1, None)
            copy_k(0)
            hi_wqk(1, 1, None)
            act.wait_ge(wqk_in[0], 16)
            a.copy(wqk_hi[:, 0, 0, :], wqk_stage[:, 0, 0, :]).then_inc(wqk_hi_done[0], 1)
            act.wait_ge(rstd_ready, 1)
            for t in range(HB):
                layer_norm(t)
            for t in range(HB):
                z_hi(t)
            copy_v(0, 0)
            for c in range(NC):
                hi_cx(1, c)
            copy_q(0)

            def second_norm(t):
                act.wait_ge(cx_second_split, t - HB + 1)
                layer_norm(t)

            unit(0, 0, first=True)
            act.wait_ge(gate_ld, 48)
            a.activation(gate[:, :], gate_in[:, :], ACT.Tanh).then_inc(gate_ready, 1)
            for t in range(HB, B):
                z_hi(t)
            for k in range(1, 4):
                unit(0, k, first=True)
            with act.Fori(1, PAIRS - 1) as p:
                for k in range(4):
                    unit(p, k)
            p = PAIRS - 1
            for k in range(3):
                unit(p, k, last=True)

            def norm_z(t):
                act.wait_ge(rstd_ready, 2 + t + 1)
                a.activation(acc[:, t, :], x_tok[:, t, :], ACT.Identity, bias=neg_mean[:, t:t + 1],
                             scale=rstd[:, t:t + 1]).then_inc(z_normed, 1)

            u = 4 * p + 3
            exps(u)
            norm_z(0)
            copy_v_bank(2 * p + 1, 1, 0)
            norm_z(1)
            norm_z(2)
            copy_v_bank(2 * p + 1, 1, 1)
            z_hi(B)
            z_hi(B + 1)
            norm_z(3)
            attended_hi(u - 1, 0)
            z_hi(B + 2)
            attended_hi(u, 1)
            z_hi(B + 3)
            norm_z(4)
            norm_z(5)
            z_hi(B + 4)
            norm_z(6)
            z_hi(B + 5)
            norm_z(7)
            z_hi(B + 6)
            z_hi(B + 7)

        @block.vector
        def _(dve):
            v = nc.vector
            step = [0]

            def link(ins):
                step[0] += 1
                ins.then_inc(vec_step, 1)
                dve.wait_ge(vec_step, step[0])

            def stats(t):
                link(v.bn_stats(bn[:, t, :], x_tok[:, t, :]))
                return v.bn_aggr(mean_var[:, t, :], bn[:, t, :])

            def z_lo(n):
                dve.wait_ge(z_hi_done, n + 1)
                o = xn_lo[:, :, tokens(n % B)]
                v.tensor_tensor(o, turned(n)[:, :].rearrange("p (c n) -> p c n", c=NC),
                                as_f32(xn_hi[:, :, tokens(n % B)]), ALU.subtract).then_inc(z_split, 1)

            def scale_x(t):
                dve.wait_ge(y_done, t + 1)
                if t == 0:
                    dve.wait_ge(ln_w_in, 16)
                if t >= HB:
                    dve.wait_ge(z_turned, max(t - 1, HB))
                v.scalar_tensor_tensor(out=xs[t], in0=acc[:, t, :], scalar=rms[:, t:t + 1],
                                       in1=ln_w_b[:, :], op0=ALU.mult, op1=ALU.mult).then_inc(xs_done, 1)

            def lo(hi_done, n, out_lo, whole, hi, done):
                dve.wait_ge(hi_done, n)
                v.tensor_tensor(out_lo, whole, as_f32(hi), ALU.subtract).then_inc(done, 1)

            def lo_wqk(n, j):
                lo(wqk_hi_done[j], n, wqk_lo[:, j, :, :], wqk_stage[:, j, :, :], wqk_hi[:, j, :, :], wqk_split[j])

            def lo_wv(n):
                lo(wv_hi_done, n, wv_lo[:, :, :], wv_stage[:, :, :], wv_hi[:, :, :], wv_split)

            def lo_wo(n):
                lo(wo_hi_done, n, wo_lo[:, :, :], wo_stage[:, :, :], wo_hi[:, :, :], wo_split)

            def attended_lo(u, j):
                lo(at_hi_done, u + 1, at_lo[:, j, :], ps_pv[:, :], at_hi[:, j, :], at_split)

            def softmax_in(u, j):
                dve.wait_ge(s_done, u + 1)
                dve.wait_ge(bm_ready, u + 1)
                if not (isinstance(u, int) and u == 0):
                    dve.wait_ge(exp_done, u)
                    dve.wait_ge(p_turned, u)
                v.tensor_tensor(scores_b, ps_s[:, :].rearrange("p (b n) -> p b n", b=HB),
                                bias_mask[:, j, :, :], ALU.add).then_inc(s_biased, 1)
                dve.wait_ge(s_biased, u + 1)
                v.tensor_reduce(neg_max_t[:, :], scores_b, AX.X, ALU.max, negate=True).then_inc(neg_max, 1)

            def softmax_out(u, s):
                dve.wait_ge(exp_done, u + 1)
                v.reciprocal(row_inv[:, :], row_sum[:, :]).then_inc(row_inv_done, 1)
                dve.wait_ge(row_inv_done, u + 1)
                v.tensor_tensor(row_inv[:, :], row_inv[:, :], row_used[:, s * HB:(s + 1) * HB], ALU.mult).then_inc(row_scale, 1)
                dve.wait_ge(row_scale, u + 1)
                v.tensor_tensor(scores[:, :].rearrange("p (j b r) -> p b j r", j=NSQ, b=HB),
                                prob[:, :].rearrange("p (b j r) -> p b j r", j=NSQ, b=HB),
                                row_inv[:, :].unsqueeze(2).unsqueeze(3).to_broadcast([P, HB, NSQ, SQ]),
                                ALU.mult).then_inc(p_norm, 1)
                dve.wait_ge(p_norm, u + 1)
                v.transpose(prob[:, :], scores[:, :]).then_inc(p_turned, 1)

            def add_out(done, s, b):
                dve.wait_ge(o_done, done + 1)
                t = s * HB + b
                v.tensor_tensor(acc[:, t, :], ps_x[b % 2][:, :], acc[:, t, :], ALU.add).then_inc(o_added, 1)

            def unit(p, k, first=False, last=False):
                u, s, j = 4 * p + k, k // 2, k % 2
                out_from = None if k % 2 == 0 or (first and k == 1) else 8 * p - 6 + 2 * k
                softmax_in(u, j)
                if first and k == 0:
                    rows_used()
                    neg_means(1)
                elif k % 2 == 0:
                    attended_lo(u - 2, 0)
                if out_from is not None:
                    add_out(out_from, 1 - s, 0)
                softmax_out(u, s)
                if out_from is not None:
                    add_out(out_from + 1, 1 - s, 1)
                if k == 2:
                    lo_wo(p + 1)
                    if not last:
                        lo_wqk(p + 2, 0)
                if k == 3:
                    lo_wqk(p + 2, 1)
                    lo_wv(p + 2)
                if out_from is not None:
                    add_out(out_from + 2, 1 - s, 2)
                    add_out(out_from + 3, 1 - s, 3)
                if k % 2 == 0 and not (first and k == 0):
                    attended_lo(u - 1, 1)
                if last and k % 2 == 0:
                    for t in range(k // 2 * HB, (k // 2 + 1) * HB):
                        gate_x(t)
                if last and k < 2:
                    for c in ((0, 1), (2,))[k]:
                        merged(c)

            def gate_x(t):
                if t == 0:
                    dve.wait_ge(gate_ready, 1)
                dve.wait_ge(o_added, 8 * PAIRS - 12 + t // HB * HB)
                v.scalar_tensor_tensor(out=x_tok[:, t, :], in0=acc[:, t, :], scalar=gate[:, 0:1],
                                       in1=x_tok[:, t, :], op0=ALU.mult, op1=ALU.add).then_inc(x_gated, 1)

            def merged(c):
                if c == 0:
                    dve.wait_ge(wf_in, 16)
                dve.wait_ge(m_done, c + 1)
                v.tensor_tensor(wf[:, c, :], ps_z[:, :], wf[:, c, :], ALU.add).then_inc(m_added, 1)
                lo(m_hi_done, c + 1, wf_lo[:, c, :], wf[:, c, :], wf_hi[:, c, :], m_split)

            def lo_cx(c):
                lo(cx_hi_done, c + 1, cx_lo[:, c, half(0)], ctx_stage[0][:, c, :], cx_hi[:, c, half(0)], cx_first_split)

            def tile_stats(t):
                dve.wait_ge(x_in[t], 16)
                link(stats(t))

            def half_stats(s):
                h = slice(s * HB, (s + 1) * HB)
                link(v.tensor_scalar(ve[:, h], mean_var[:, h, 1], EPS, None, ALU.add))
                link(v.reciprocal(ve_inv[:, h], ve[:, h]))
                link(v.tensor_tensor(ve_inv[:, h], ve_inv[:, h], mean_var[:, h, 1], ALU.mult))
                v.tensor_scalar(rms_in[:, h], ve_inv[:, h], EPS, None, ALU.add).then_inc(norm_in_ready, 1)

            def neg_means(s):
                h = slice(s * HB, (s + 1) * HB)
                dve.wait_ge(norm_out_ready, s + 1)
                v.scalar_tensor_tensor(out=neg_mean[:, h], in0=mean_var[:, h, 0], scalar=-1.0,
                                       in1=rstd[:, h], op0=ALU.mult, op1=ALU.mult).then_inc(rstd_ready, 1)

            lo_cx(0)
            lo(first_k_hi, 1, wqk_lo[:, 0, 1, :], wqk_stage[:, 0, 1, :], wqk_hi[:, 0, 1, :], first_k_split)
            for c in range(1, NC):
                lo_cx(c)
            lo(wv_hi_done, 1, wv_lo[:, :NC // 2, :], wv_stage[:, :NC // 2, :], wv_hi[:, :NC // 2, :], wv_split)
            for t in range(HB):
                tile_stats(t)
            half_stats(0)
            lo_wqk(1, 1)
            lo(wqk_hi_done[0], 1, wqk_lo[:, 0, 0, :], wqk_stage[:, 0, 0, :], wqk_hi[:, 0, 0, :], wqk_split[0])
            neg_means(0)
            for t in range(HB):
                scale_x(t)
            for t in range(HB):
                z_lo(t)
            for t in range(HB, B):
                tile_stats(t)
            half_stats(1)

            def rows_used():
                dve.wait_ge(mask_ready, 1)
                link(v.tensor_reduce(row_best[:, :], mask_add[:, :, :], AX.X, ALU.max))
                v.tensor_scalar(row_used[:, :], row_best[:, :], -0.5 * MASKED, None, ALU.is_ge).then_inc(used_ready, 1)
                dve.wait_ge(used_ready, 1)

            unit(0, 0, first=True)
            scale_x(4)
            scale_x(5)
            z_lo(4)
            scale_x(6)
            z_lo(5)
            scale_x(7)
            z_lo(6)
            z_lo(7)
            for k in range(1, 4):
                unit(0, k, first=True)
            with dve.Fori(1, PAIRS - 1) as p:
                for k in range(4):
                    unit(p, k)
            p = PAIRS - 1
            for k in range(3):
                unit(p, k, last=True)

            def gate_out(t):
                dve.wait_ge(x_gated, t + 1)
                dve.wait_ge(o_done, 8 * PAIRS - 8 + t + 1)
                v.scalar_tensor_tensor(out=x_tok[:, t, :], in0=ps_x[t % 2][:, :], scalar=gate[:, 0:1],
                                       in1=x_tok[:, t, :], op0=ALU.mult, op1=ALU.add).then_inc(o_added, 1)
                dve.wait_ge(o_added, 8 * PAIRS - 8 + t + 1)
                stats(t).then_inc(x2_done, 1)

            def result(t):
                dve.wait_ge(f_done, t + 1)
                dve.wait_ge(x2_biased, t + 1)
                v.scalar_tensor_tensor(out=acc[:, t, :], in0=ps_f[t % 2][:, :], scalar=gate[:, 1:2],
                                       in1=x_tok[:, t, :], op0=ALU.mult, op1=ALU.add).then_inc(f_out, 1)

            u = 4 * p + 3
            softmax_in(u, 1)
            merged(3)
            gate_out(0)
            softmax_out(u, 1)
            for t in range(1, HB):
                gate_out(t)
            z_lo(B)
            z_lo(B + 1)
            attended_lo(u - 1, 0)
            z_lo(B + 2)
            result(0)
            attended_lo(u, 1)
            z_lo(B + 3)
            gate_out(4)
            result(1)
            gate_out(5)
            gate_out(6)
            gate_out(7)
            for t in range(4, B):
                z_lo(B + t)
                result(t - 2)
            result(B - 2)
            result(B - 1)


def kernel(x, ctx_4096, mask_BxSxS2_bk0, g_xattn, g_ffn, L0_xattn_position_bias, L0_xattn_ln_weight,
           L0_xattn_w_q, L0_xattn_w_k, L0_xattn_w_v, L0_xattn_w_out, L0_ffn_lora_A, L0_ffn_lora_B,
           L0_ffn_W, L0_ffn_bias, L0_ffn_lora_weights):
    import numpy as np
    import concourse.bacc as bacc
    from concourse.bass_utils import run_bass_kernel_spmd

    def laid(a, shape, axes, to):
        return np.ascontiguousarray(np.asarray(a).reshape(shape).transpose(axes).reshape(to))

    arrays = {
        "x": np.ascontiguousarray(x),
        "ctx_t": laid(ctx_4096, (2, HT, NC, P), (0, 3, 2, 1), (2, P, NC, HT)),
        "mask": np.ascontiguousarray(np.asarray(mask_BxSxS2_bk0).transpose(1, 0, 2)),
        "g_xattn": np.ascontiguousarray(g_xattn),
        "g_ffn": np.ascontiguousarray(g_ffn),
        "bias": laid(L0_xattn_position_bias, (PAIRS, 2, S, S), (0, 2, 1, 3), (PAIRS, S, 2, S)),
        "ln_w": np.ascontiguousarray(L0_xattn_ln_weight),
        "wq": laid(L0_xattn_w_q, (H, DH, NC, P), (0, 3, 2, 1), (H, P, NC * DH)),
        "wk": laid(L0_xattn_w_k, (H, DH, NC, P), (0, 3, 2, 1), (H, P, NC * DH)),
        "wv": laid(L0_xattn_w_v, (PAIRS, 2 * DH, NC, P), (0, 3, 2, 1), (PAIRS, P, NC, 2 * DH)),
        "wo": laid(L0_xattn_w_out, (D, PAIRS, 2, DH), (1, 3, 2, 0), (PAIRS, DH, 2, D)),
        "lora_a": laid(L0_ffn_lora_A, (N_LORA * RANK, D), (0, 1), (N_LORA * RANK, D)),
        "lora_bt": laid(L0_ffn_lora_B, (N_LORA, D, RANK), (0, 2, 1), (N_LORA * RANK, D)),
        "w_t": laid(L0_ffn_W, (D, NC, P), (2, 1, 0), (P, NC, D)),
        "ffn_bias": np.ascontiguousarray(L0_ffn_bias),
        "lora_w": np.repeat(np.asarray(L0_ffn_lora_weights), RANK).reshape(P, 1),
    }
    nc = bacc.Bacc("TRN2", target_bir_lowering=False, num_devices=1)
    args = [nc.dram_tensor(f"{name}_dram", a.shape, mybir.dt.from_np(a.dtype), kind="ExternalInput").ap()
            for name, a in arrays.items()]
    out = nc.dram_tensor("out_dram", (B, S, D), FP32, kind="ExternalOutput").ap()
    gated_block(nc, *args, out)
    r = run_bass_kernel_spmd(nc, [{f"{name}_dram": a for name, a in arrays.items()}], core_ids=[0])
    return r.results[0]["out_dram"]
```

```python
import concourse.bass as bass
from concourse import mybir
from contextlib import ExitStack

FP32 = mybir.dt.float32
FP32R = mybir.dt.float32r
U8 = mybir.dt.uint8
ALU = mybir.AluOpType
ACT = mybir.ActivationFunctionType
AX = mybir.AxisListType

B, S, D = 8, 128, 512
H, DH = 32, 128
P = 128
NC = D // P
HB = B // 2
HT = HB * S
PAIRS = H // 2
N_LORA, RANK = 8, 16
EPS = 1e-5
SQ = 32
NSQ = S // SQ
OWN = HB - 1
WARM_UP = 9
LORA_SCALE = 2.0
MASKED = 1e30


def gated_block(nc, x, ctx_t, mask, g_xattn, g_ffn, bias, ln_w, wq, wk, wv, wo,
                lora_a, lora_bt, w_t, ffn_bias, lora_w, out):
    stack = ExitStack()
    with stack:
        def sb(name, shape, dt=FP32):
            return stack.enter_context(nc.sbuf_tensor(name, shape, dt))

        def ps(name):
            return stack.enter_context(nc.psum_tensor(name, [P, 512], FP32))

        def sem(name):
            return stack.enter_context(nc.semaphore(name))

        x_tok = sb("x_tok", [P, B, D])
        acc = sb("acc", [P, B, D])
        xn_hi = sb("xn_hi", [P, NC, B * S], FP32R)
        xn_lo = sb("xn_lo", [P, NC, B * S], FP32R)
        cx_hi = sb("cx_hi", [P, NC, B * S], FP32R)
        cx_lo = sb("cx_lo", [P, NC, B * S], FP32R)
        wqk_stage = sb("wqk_stage", [P, 2, 2, D])
        wqk_hi = sb("wqk_hi", [P, 2, 2, D], FP32R)
        wqk_lo = sb("wqk_lo", [P, 2, 2, D], FP32R)
        wv_stage = sb("wv_stage", [P, NC, 2 * DH])
        wv_hi = sb("wv_hi", [P, NC, 2 * DH], FP32R)
        wv_lo = sb("wv_lo", [P, NC, 2 * DH], FP32R)
        wo_stage = sb("wo_stage", [P, 2, D])
        wo_hi = sb("wo_hi", [P, 2, D], FP32R)
        wo_lo = sb("wo_lo", [P, 2, D], FP32R)
        q_t = sb("q_t", [P, HT])
        k_t = sb("k_t", [P, HT])
        v_tok = sb("v_tok", [P, 2, HB, 2 * DH])
        at_hi = sb("at_hi", [P, 2, HT], FP32R)
        at_lo = sb("at_lo", [P, 2, HT], FP32R)
        scores = sb("scores", [P, HT])
        prob = sb("prob", [P, HT])
        prob_t = sb("prob_t", [P, 2, HT])
        prob_dram = nc.dram_tensor("prob_scratch", (2, P, HT), FP32).ap()
        bias_stage = sb("bias_stage", [P, 2, S])
        bias_mask = sb("bias_mask", [P, 2, HB, S])
        mask_u8 = sb("mask_u8", [P, B, S], U8)
        mask_add = sb("mask_add", [P, B, S])
        row_used = sb("row_used", [P, B])
        row_best = sb("row_best", [P, B])
        neg_max_t = sb("neg_max_t", [P, HB])
        row_sum = sb("row_sum", [P, HB])
        row_inv = sb("row_inv", [P, HB])
        ident = sb("ident", [P, P])
        neg_half = sb("neg_half", [P, 2, HB])
        ln_w_b = sb("ln_w_b", [P, D])
        ffn_bias_b = sb("ffn_bias_b", [P, D])
        bn = sb("bn", [P, B, 6])
        mean_var = sb("mean_var", [P, B, 2])
        norm_in = sb("norm_in", [P, 2, B])
        norm_out = sb("norm_out", [P, 2, B])
        norm_v = sb("norm_v", [P, 2, B])
        gate_in = sb("gate_in", [P, 2])
        gate = sb("gate", [P, 2])
        lora_w_col = sb("lora_w_col", [P, 1])
        lora_a_sb = sb("lora_a_sb", [P, D])
        lora_b_sb = sb("lora_b_sb", [P, D])
        wf_hi = sb("wf_hi", [P, NC, D], FP32R)
        wf_lo = sb("wf_lo", [P, NC, D], FP32R)
        wf = wqk_stage[:, :, :, :].rearrange("p a b n -> p (a b) n")
        scores_b, prob_b = (t[:, :].rearrange("p (b n) -> p b n", b=HB) for t in (scores, prob))
        ve, rms_in, rstd, rms = norm_in[:, 0, :], norm_in[:, 1, :], norm_out[:, 0, :], norm_out[:, 1, :]
        ve_inv, neg_mean = norm_v[:, 0, :], norm_v[:, 1, :]

        ps_s, ps_q, ps_k, ps_t, ps_pv, ps_z = (ps(n) for n in ("ps_s", "ps_q", "ps_k", "ps_t", "ps_pv", "ps_z"))
        ps_x = [ps("ps_x0"), ps("ps_x1")]
        ps_f = [ps_q, ps_k]

        x_in = [sem(f"x_in{t}") for t in range(B)]
        cx_first_in = [sem(f"cx_first_in{c}") for c in range(NC)]
        cx_second_in, first_k_in = sem("cx_second_in"), sem("first_k_in")
        wqk_in = [sem(f"wqk_in{j}") for j in range(2)]
        wv_in, wo_in, bias_in, mask_in = sem("wv_in"), sem("wo_in"), sem("bias_in"), sem("mask_in")
        gate_ld, ln_w_in, lora_in, wf_in = sem("gate_ld"), sem("ln_w_in"), sem("lora_in"), sem("wf_in")
        out_stored = sem("out_stored")
        cx_hi_done, cx_first_split = sem("cx_hi_done"), sem("cx_first_split")
        cx_second_split, cx_second_rest = sem("cx_second_split"), sem("cx_second_rest")
        first_k_hi, first_k_split, first_v_rest = sem("first_k_hi"), sem("first_k_split"), sem("first_v_rest")
        wqk_hi_done = [sem(f"wqk_hi_done{j}") for j in range(2)]
        wqk_split = [sem(f"wqk_split{j}") for j in range(2)]
        wv_hi_done, wv_split, wo_hi_done, wo_split = (sem(n) for n in ("wv_hi_done", "wv_split", "wo_hi_done", "wo_split"))
        consts = sem("consts")
        norm_in_ready, norm_out_ready = sem("norm_in_ready"), sem("norm_out_ready")
        rstd_ready, y_done, xs_done = (sem(n) for n in ("rstd_ready", "y_done", "xs_done"))
        own_y_done = sem("own_y_done")
        z_turned, z_hi_done, z_split = sem("z_turned"), sem("z_hi_done"), sem("z_split")
        pool_step, vec_step = sem("pool_step"), sem("vec_step")
        q_done, q_copied, k_done, k_copied = (sem(n) for n in ("q_done", "q_copied", "k_done", "k_copied"))
        s_done, bm_ready, s_biased, neg_max, exp_done, row_inv_done, row_scale, p_norm, p_turned, p_sent = (
            sem(n) for n in ("s_done", "bm_ready", "s_biased", "neg_max", "exp_done", "row_inv_done", "row_scale", "p_norm", "p_turned", "p_sent"))
        pv_done, at_hi_done, at_split = (sem(n) for n in ("pv_done", "at_hi_done", "at_split"))
        pt_in = [sem(f"pt_in{i}") for i in range(2)]
        v_done, v_copied = sem("v_done"), sem("v_copied")
        o_done, o_added = sem("o_done"), sem("o_added")
        gate_ready, mask_ready, used_ready = sem("gate_ready"), sem("mask_ready"), sem("used_ready")
        lora_scaled, m_done, m_added, m_hi_done, m_split = (sem(n) for n in ("lora_scaled", "m_done", "m_added", "m_hi_done", "m_split"))
        x_gated = sem("x_gated")
        bias_gated, x2_done, z_normed, x2_biased, f_done, f_out = (
            sem(n) for n in ("bias_gated", "x2_done", "z_normed", "x2_biased", "f_done", "f_out"))

        block = stack.enter_context(nc.Block())

        def as_f32(ap):
            return ap.bitcast(FP32)

        ctx_stage = [v_tok[:, :, :, :].rearrange("p s b n -> p (s b n)").rearrange("p (c n) -> p c n", c=NC),
                     acc[:, HB:B, :]]
        xs = [lora_a_sb[:, :], lora_b_sb[:, :], scores[:, :], prob[:, :]] + [lora_a_sb[:, :], lora_b_sb[:, :]] * 2

        def turned(n):
            if n < HB:
                return (ps_z, ps_pv, ps_s, ps_t)[n]
            return ps_z if (n + n // B) % 2 == 0 else ps_t

        def tokens(t):
            return slice(t * S, (t + 1) * S)

        def half(s):
            return slice(s * HT, (s + 1) * HT)

        @block.sync
        def _(sp):
            def load_wqk(p, j):
                sp.dma_start(wqk_stage[:, j, 0, :], wq[2 * p + j]).then_inc(wqk_in[j], 16)
                sp.dma_start(wqk_stage[:, j, 1, :], wk[2 * p + j]).then_inc(wqk_in[j], 16)

            sp.dma_start(ctx_stage[0][:, 0, :], ctx_t[0, :, 0, :]).then_inc(cx_first_in[0], 16)
            sp.dma_start(wqk_stage[:, 0, 1, :], wk[0]).then_inc(first_k_in, 16)
            for c in range(1, NC):
                sp.dma_start(ctx_stage[0][:, c, :], ctx_t[0, :, c, :]).then_inc(cx_first_in[c], 16)
            sp.dma_start(wv_stage[:, :, :], wv[0]).then_inc(wv_in, 16)
            for t in range(HB):
                sp.dma_start(x_tok[:, t, :], x[t]).then_inc(x_in[t], 16)
            load_wqk(0, 1)
            sp.dma_start(ln_w_b[:, :], ln_w.partition_broadcast(P)).then_inc(ln_w_in, 16)
            sp.dma_start(wqk_stage[:, 0, 0, :], wq[0]).then_inc(wqk_in[0], 16)
            for t in range(HB, B):
                sp.dma_start(x_tok[:, t, :], x[t]).then_inc(x_in[t], 16)
            sp.dma_start(mask_u8[:, :, :], mask).then_inc(mask_in, 16)
            sp.dma_start(bias_stage[:, :, :], bias[0]).then_inc(bias_in, 16)
            sp.dma_start(ctx_stage[1], ctx_t[1]).then_inc(cx_second_in, 16)
            sp.dma_start(wo_stage[:, :, :], wo[0]).then_inc(wo_in, 16)
            sp.dma_start(gate_in[:, 0:1], g_xattn.partition_broadcast(P)).then_inc(gate_ld, 16)
            sp.dma_start(gate_in[:, 1:2], g_ffn.partition_broadcast(P)).then_inc(gate_ld, 16)
            sp.dma_start(ffn_bias_b[:, :], ffn_bias.partition_broadcast(P)).then_inc(gate_ld, 16)

            def move_probs(p, k):
                u = 4 * p + k
                sp.wait_ge(p_turned, u + 1)
                sp.dma_start(prob_dram[k % 2], prob[:, :]).then_inc(p_sent, 16)
                sp.wait_ge(p_sent, 16 * (u + 1))
                for j in range(NSQ):
                    sp.dma_start(prob_t[j * SQ:(j + 1) * SQ, k % 2, :].rearrange("a (i r) -> a i r", i=NSQ),
                                 prob_dram[k % 2, :, j * P:(j + 1) * P].rearrange("(i a) r -> a i r", a=SQ)).then_inc(pt_in[k % 2], 16)

            def prefetch(p, k):
                if k == 0:
                    sp.wait_ge(wqk_split[0], p + 1)
                    load_wqk(p + 1, 0)
                if k == 1:
                    sp.wait_ge(wqk_split[1], p + 1)
                    load_wqk(p + 1, 1)
                    sp.wait_ge(wv_split, p + 1)
                    sp.dma_start(wv_stage[:, :, :], wv[p + 1]).then_inc(wv_in, 16)
                if k == 2:
                    sp.wait_ge(bm_ready, 4 * p + 4)
                    sp.dma_start(bias_stage[:, :, :], bias[p + 1]).then_inc(bias_in, 16)
                if k == 3:
                    sp.wait_ge(wo_split, p + 1)
                    sp.dma_start(wo_stage[:, :, :], wo[p + 1]).then_inc(wo_in, 16)

            sp.wait_ge(first_v_rest, 1)
            for k in range(4):
                move_probs(0, k)
                prefetch(0, k)
            sp.wait_ge(z_turned, B)
            sp.dma_start(lora_a_sb[:, :], lora_a).then_inc(lora_in, 16)
            sp.dma_start(lora_b_sb[:, :], lora_bt).then_inc(lora_in, 16)
            sp.dma_start(lora_w_col[:, :], lora_w).then_inc(lora_in, 16)
            with sp.Fori(1, PAIRS - 1) as p:
                for k in range(4):
                    move_probs(p, k)
                    prefetch(p, k)
            for j in range(2):
                sp.wait_ge(wqk_split[j], PAIRS)
            sp.dma_start(wf, w_t).then_inc(wf_in, 16)
            for k in range(4):
                move_probs(PAIRS - 1, k)
            for t in range(B):
                sp.wait_ge(f_out, t + 1)
                sp.dma_start(out[t], acc[:, t, :]).then_inc(out_stored, 16)
            sp.wait_ge(out_stored, 16 * B)

        @block.gpsimd
        def _(pool):
            step = [0]

            def link(ins):
                step[0] += 1
                ins.then_inc(pool_step, 1)
                pool.wait_ge(pool_step, step[0])

            g = nc.gpsimd
            link(g.memset(ident[:, :], 0.0))
            link(g.affine_select(out=ident[:, :], in_=ident[:, :], compare_op=ALU.not_equal, fill=1.0,
                                 base=0, pattern=[[-1, P]], channel_multiplier=1))
            g.memset(neg_half[:, :, :], -0.5).then_inc(consts, 1)
            pool.wait_ge(consts, 1)

            def norm_scales(s):
                h = slice(s * HB, (s + 1) * HB)
                pool.wait_ge(norm_in_ready, s + 1)
                g.tensor_tensor(out=norm_out[:, :, h], in0=norm_in[:, :, h], in1=neg_half[:, :, :],
                                op=ALU.pow).then_inc(norm_out_ready, 1)

            def bias_and_mask(p, k):
                s, j = k // 2, k % 2
                if k == 0:
                    pool.wait_ge(bias_in, 16 * (p + 1))
                if not (isinstance(p, int) and 4 * p + k < 2):
                    pool.wait_ge(s_biased, 4 * p + k - 1)
                g.tensor_tensor(out=bias_mask[:, j, :, :],
                                in0=bias_stage[:, j, :].unsqueeze(1).to_broadcast([P, HB, S]),
                                in1=mask_add[:, s * HB:(s + 1) * HB, :], op=ALU.add).then_inc(bm_ready, 1)

            pool.wait_ge(wv_hi_done, 1)
            g.tensor_tensor(out=wv_lo[:, NC // 2:, :], in0=wv_stage[:, NC // 2:, :],
                            in1=as_f32(wv_hi[:, NC // 2:, :]), op=ALU.subtract).then_inc(first_v_rest, 1)
            norm_scales(0)
            pool.wait_ge(rstd_ready, 1)
            g.tensor_scalar(acc[:, OWN, :], x_tok[:, OWN, :], rstd[:, OWN:OWN + 1], neg_mean[:, OWN:OWN + 1],
                            ALU.mult, ALU.add).then_inc(own_y_done, 1)
            pool.wait_ge(wqk_hi_done[0], 1)
            g.tensor_tensor(out=wqk_lo[:, 0, 0, :], in0=wqk_stage[:, 0, 0, :],
                            in1=as_f32(wqk_hi[:, 0, 0, :]), op=ALU.subtract).then_inc(wqk_split[0], 1)
            pool.wait_ge(mask_in, 16)
            g.tensor_scalar(mask_add[:, :, :], mask_u8[:, :, :], MASKED, -MASKED, ALU.mult, ALU.add).then_inc(mask_ready, 1)
            pool.wait_ge(mask_ready, 1)
            bias_and_mask(0, 0)
            for c in range(NC // 2):
                pool.wait_ge(cx_hi_done, NC + c + 1)
                g.tensor_tensor(out=cx_lo[:, c, half(1)], in0=ctx_stage[1][:, c, :],
                                in1=as_f32(cx_hi[:, c, half(1)]), op=ALU.subtract).then_inc(cx_second_split, 1)
            norm_scales(1)
            for k in range(1, 4):
                bias_and_mask(0, k)
            with pool.Fori(1, PAIRS - 1) as p:
                for k in range(4):
                    bias_and_mask(p, k)

            pool.wait_ge(lora_in, 48)
            g.tensor_scalar(lora_b_sb[:, :], lora_b_sb[:, :], lora_w_col[:, 0:1], LORA_SCALE,
                            ALU.mult, ALU.mult).then_inc(lora_scaled, 1)
            pool.wait_ge(gate_ready, 1)
            g.tensor_scalar(ffn_bias_b[:, :], ffn_bias_b[:, :], gate[:, 1:2], 1.0,
                            ALU.mult, ALU.mult).then_inc(bias_gated, 1)
            pool.wait_ge(bias_gated, 1)

            for k in range(4):
                bias_and_mask(PAIRS - 1, k)

            def x2_scale(t):
                pool.wait_ge(x2_done, t + 1)
                link(g.tensor_scalar(ve[:, t:t + 1], mean_var[:, t, 1:2], EPS, None, ALU.add))
                link(g.tensor_tensor(out=rstd[:, t:t + 1], in0=ve[:, t:t + 1], in1=neg_half[:, 0, 0:1], op=ALU.pow))
                g.tensor_scalar(neg_mean[:, t:t + 1], mean_var[:, t, 0:1], rstd[:, t:t + 1], -1.0,
                                ALU.mult, ALU.mult).then_inc(rstd_ready, 1)

            def x2_bias(t):
                pool.wait_ge(z_normed, t + 1)
                g.tensor_tensor(out=x_tok[:, t, :], in0=x_tok[:, t, :], in1=ffn_bias_b[:, :],
                                op=ALU.add).then_inc(x2_biased, 1)

            for s in range(2):
                for t in range(s * HB, (s + 1) * HB):
                    x2_scale(t)
                for t in range(s * HB, (s + 1) * HB):
                    x2_bias(t)

        @block.tensor
        def _(pe):
            def three(o, l_hi, l_lo, r_hi, r_lo, start, stop):
                nc.tensor.matmul(o, l_hi, r_hi, start=start, stop=False)
                nc.tensor.matmul(o, l_hi, r_lo, start=False, stop=False)
                return nc.tensor.matmul(o, l_lo, r_hi, start=False, stop=stop)

            def project(k, key, arriving=False):
                s, j = k // 2, k % 2
                o, r_hi, r_lo = (ps_k, cx_hi, cx_lo) if key else (ps_q, xn_hi, xn_lo)
                for c in range(NC):
                    if arriving:
                        pe.wait_ge(cx_first_split, c + 1)
                    w = slice(c * DH, (c + 1) * DH)
                    last = three(o[:, :], wqk_hi[:, j, int(key), w], wqk_lo[:, j, int(key), w],
                                 r_hi[:, c, half(s)], r_lo[:, c, half(s)], c == 0, c == NC - 1)
                last.then_inc(k_done if key else q_done, 1)

            def values_bank(s, i):
                for b in (2 * i, 2 * i + 1):
                    o = ps_x[i][:, (b % 2) * 2 * DH:(b % 2 + 1) * 2 * DH]
                    for c in range(NC):
                        last = three(o, cx_hi[:, c, tokens(s * HB + b)], cx_lo[:, c, tokens(s * HB + b)],
                                     wv_hi[:, c, :], wv_lo[:, c, :], c == 0, c == NC - 1)
                last.then_inc(v_done, 1)

            def values(s, added):
                for i in range(2):
                    pe.wait_ge(o_added, added + i)
                    values_bank(s, i)

            def turn(src, n, ready, count):
                pe.wait_ge(ready, count)
                if n >= HB:
                    pe.wait_ge(z_split, n - 1)
                for c in range(NC):
                    last = nc.tensor.transpose(turned(n)[:, c * P:(c + 1) * P], src[:, c * P:(c + 1) * P], ident[:, :])
                last.then_inc(z_turned, 1)

            def out_tile(first, b, wo_pair, units, copied=None):
                if b == 0:
                    pe.wait_ge(wo_split, wo_pair + 1)
                    pe.wait_ge(at_split, units)
                if b < 2 and copied is not None:
                    pe.wait_ge(v_copied, copied)
                else:
                    pe.wait_ge(o_added, first + b - 1)
                for j in range(2):
                    last = three(ps_x[b % 2][:, :], at_hi[:, j, tokens(b)], at_lo[:, j, tokens(b)],
                                 wo_hi[:, j, :], wo_lo[:, j, :], j == 0, j == 1)
                last.then_inc(o_done, 1)

            def score(p, k):
                u = 4 * p + k
                pe.wait_ge(q_copied, u + 1)
                pe.wait_ge(k_copied, u + 1)
                if not (isinstance(u, int) and u == 0):
                    pe.wait_ge(s_biased, u)
                for b in range(HB):
                    last = nc.tensor.matmul(ps_s[:, tokens(b)], q_t[:, tokens(b)], k_t[:, tokens(b)], start=True, stop=True)
                last.then_inc(s_done, 1)

            def attend(p, k):
                u, s, j = 4 * p + k, k % 4 // 2, k % 2
                pe.wait_ge(pt_in[k % 2], 16 * NSQ * (2 * p + k // 2 + 1))
                if j == 0:
                    pe.wait_ge(v_copied, u + 2)
                if not (isinstance(u, int) and u == 0):
                    pe.wait_ge(at_split, u)
                pt = prob_t[:, k % 2, :].rearrange("p (i b r) -> p b i r", i=NSQ, b=HB)
                for b in range(HB):
                    last = nc.tensor.matmul(ps_pv[:, tokens(b)], v_tok[:, s, b, j * DH:(j + 1) * DH],
                                            pt[:, b, :, :], start=True, stop=True)
                last.then_inc(pv_done, 1)

            def unit(p, k, first=False, last=False):
                u = 4 * p + k
                out_from = None if k % 2 == 0 else 8 * p - 6 + 2 * k
                score(p, k)
                if out_from is not None:
                    for b in range(2):
                        out_tile(out_from, b, p - (k == 1), u - 1, copied=u + 1)
                nk = (k + 1) % 4
                pe.wait_ge(wqk_split[nk % 2], p + 1 + (k == 3))
                project(nk, False)
                if not (first and k == 0):
                    project(nk, True)
                if out_from is not None:
                    for b in range(2, HB):
                        out_tile(out_from, b, p - (k == 1), u - 1)
                if not (first and k == 0):
                    attend(p, k - 1)
                if last and k == 0:
                    merge(0)
                if first and k == 2:
                    values_bank(1, 1)
                elif k % 2 == 0 and not first and not (last and k == 2):
                    pe.wait_ge(wv_split, p + 1)
                    values(k // 2, 8 * p - 5 + 2 * k)
                if last:
                    merge(k + 1)

            def merge(c):
                if c == 0:
                    pe.wait_ge(lora_scaled, 1)
                else:
                    pe.wait_ge(m_added, c)
                nc.tensor.matmul(ps_z[:, :], lora_a_sb[:, c * P:(c + 1) * P], lora_b_sb[:, :],
                                 start=True, stop=True).then_inc(m_done, 1)

            def ffn(t):
                pe.wait_ge(z_split, B + t + 1)
                if t == 0:
                    pe.wait_ge(m_split, NC)
                if t >= 2:
                    pe.wait_ge(f_out, t - 1)
                for c in range(NC):
                    last = three(ps_f[t % 2][:, :], xn_hi[:, c, tokens(t)], xn_lo[:, c, tokens(t)],
                                 wf_hi[:, c, :], wf_lo[:, c, :], c == 0, c == NC - 1)
                last.then_inc(f_done, 1)

            def turn_x(t):
                turn(xs[t], t, xs_done, t + 1)

            pe.wait_ge(consts, 1)
            for _ in range(WARM_UP):
                nc.tensor.matmul(ps_s[:, :P], ident[:, :], ident[:, :], start=True, stop=True)

            pe.wait_ge(first_k_split, 1)
            project(0, True, arriving=True)
            pe.wait_ge(wv_split, 1)
            pe.wait_ge(first_v_rest, 1)
            values_bank(0, 0)
            values_bank(0, 1)
            pe.wait_ge(wqk_split[1], 1)
            pe.wait_ge(k_copied, 1)
            project(1, True)
            for t in range(HB):
                turn_x(t)
            pe.wait_ge(wqk_split[0], 1)
            pe.wait_ge(z_split, HB)
            project(0, False)

            unit(0, 0, first=True)
            pe.wait_ge(cx_second_split, NC // 2)
            pe.wait_ge(cx_second_rest, NC // 2)
            pe.wait_ge(v_copied, 1)
            values_bank(1, 0)
            turn_x(4)
            turn_x(5)
            score(0, 1)
            turn_x(6)
            turn_x(7)
            project(2, True)
            pe.wait_ge(z_split, B)
            project(2, False)
            attend(0, 0)
            for k in range(2, 4):
                unit(0, k, first=True)
            with pe.Fori(1, PAIRS - 1) as p:
                for k in range(4):
                    unit(p, k)
            p = PAIRS - 1
            for k in range(3):
                unit(p, k, last=True)

            def turn_z(t):
                if t == 1:
                    pe.wait_ge(m_added, NC)
                turn(acc[:, t, :], B + t, z_normed, t + 1)

            score(p, 3)
            for b in range(HB):
                out_tile(8 * p, b, p, 4 * p + 2)
            values(1, 8 * p + 3)
            turn_z(0)
            turn_z(1)
            attend(p, 2)
            ffn(0)
            turn_z(2)
            attend(p, 3)
            ffn(1)
            turn_z(3)
            for b in range(HB):
                out_tile(8 * p + 4, b, p, 4 * p + 4, copied=4 * p + 4)
            for t in range(2, B):
                ffn(t)
                if t + 2 < B:
                    turn_z(t + 2)

        @block.scalar
        def _(act):
            a = nc.scalar

            def z_hi(n):
                act.wait_ge(z_turned, n + 1)
                a.copy(xn_hi[:, :, tokens(n % B)], turned(n)[:, :].rearrange("p (c n) -> p c n", c=NC)).then_inc(z_hi_done, 1)

            def copy_q(u):
                act.wait_ge(q_done, u + 1)
                if not (isinstance(u, int) and u == 0):
                    act.wait_ge(s_done, u)
                a.copy(q_t[:, :], ps_q[:, :]).then_inc(q_copied, 1)

            def copy_k(u):
                act.wait_ge(k_done, u + 1)
                if not (isinstance(u, int) and u == 0):
                    act.wait_ge(s_done, u)
                a.copy(k_t[:, :], ps_k[:, :]).then_inc(k_copied, 1)

            def copy_v_bank(blocks, s, i):
                act.wait_ge(v_done, 2 * blocks + i + 1)
                a.copy(v_tok[:, s, 2 * i:2 * i + 2, :].rearrange("p b n -> p (b n)"), ps_x[i][:, :]).then_inc(v_copied, 1)

            def copy_v(blocks, s):
                for i in range(2):
                    copy_v_bank(blocks, s, i)

            def attended_hi(u, j):
                act.wait_ge(pv_done, u + 1)
                a.copy(at_hi[:, j, :], ps_pv[:, :]).then_inc(at_hi_done, 1)

            def exps(u):
                act.wait_ge(neg_max, u + 1)
                if not (isinstance(u, int) and u == 0):
                    act.wait_ge(p_sent, 16 * u)
                for b in range(HB):
                    last = a.activation(prob[:, tokens(b)], scores[:, tokens(b)], ACT.Exp, bias=neg_max_t[:, b:b + 1],
                                        scale=1.0, accum_out=row_sum[:, b:b + 1])
                last.then_inc(exp_done, 1)

            def hi_wqk(n, j, used):
                act.wait_ge(wqk_in[j], 32 * n - 16 * (j == 0))
                if used is not None:
                    act.wait_ge(k_done, used)
                a.copy(wqk_hi[:, j, :, :], wqk_stage[:, j, :, :]).then_inc(wqk_hi_done[j], 1)

            def hi_wv(n, used):
                act.wait_ge(wv_in, 16 * n)
                if used is not None:
                    act.wait_ge(v_done, used)
                a.copy(wv_hi[:, :, :], wv_stage[:, :, :]).then_inc(wv_hi_done, 1)

            def hi_wo(n, used):
                act.wait_ge(wo_in, 16 * n)
                if used is not None:
                    act.wait_ge(o_done, used)
                a.copy(wo_hi[:, :, :], wo_stage[:, :, :]).then_inc(wo_hi_done, 1)

            def hi_cx(s, c):
                act.wait_ge(cx_second_in if s else cx_first_in[c], 16)
                a.copy(cx_hi[:, c, half(s)], ctx_stage[s][:, c, :]).then_inc(cx_hi_done, 1)

            def layer_norm(t):
                a.activation(acc[:, t, :], x_tok[:, t, :], ACT.Identity, bias=neg_mean[:, t:t + 1],
                             scale=rstd[:, t:t + 1]).then_inc(y_done, 1)

            def weights_hi(p, k, first):
                if k == 2:
                    hi_wo(p + 1, None if first else 8 * p)
                    hi_wqk(p + 2, 0, 4 * p + 3)
                if k == 3:
                    hi_wqk(p + 2, 1, 4 * p + 4)
                    hi_wv(p + 2, 4 * p + 4)

            def unit(p, k, first=False, last=False):
                u = 4 * p + k
                if k % 2 == 0:
                    attended_hi(u - 2, 0)
                exps(u)
                if last and k == 2:
                    hi_wo(p + 1, 8 * p)
                if not last:
                    weights_hi(p, k, first)
                copy_q(u + 1)
                copy_k(u + 1)
                if k % 2 == 0:
                    attended_hi(u - 1, 1)
                    if last and k == 0:
                        merged_hi(0)
                    if first:
                        copy_v_bank(1, 1, 1)
                    elif not (last and k == 2):
                        copy_v(2 * p + k // 2, k // 2)
                if last and k < 2:
                    merged_hi(k + 1)

            def merged_hi(c):
                act.wait_ge(m_added, c + 1)
                a.copy(wf_hi[:, c, :], wf[:, c, :]).then_inc(m_hi_done, 1)

            hi_cx(0, 0)
            act.wait_ge(first_k_in, 16)
            a.copy(wqk_hi[:, 0, 1, :], wqk_stage[:, 0, 1, :]).then_inc(first_k_hi, 1)
            for c in range(1, NC):
                hi_cx(0, c)
            hi_wv(1, None)
            copy_k(0)
            hi_wqk(1, 1, None)
            act.wait_ge(wqk_in[0], 16)
            a.copy(wqk_hi[:, 0, 0, :], wqk_stage[:, 0, 0, :]).then_inc(wqk_hi_done[0], 1)
            act.wait_ge(rstd_ready, 1)
            for t in range(OWN):
                layer_norm(t)
            for t in range(HB):
                z_hi(t)
            copy_v(0, 0)
            for c in range(NC):
                hi_cx(1, c)
            copy_q(0)

            def second_norm(t):
                c = t - HB
                if c < NC // 2:
                    act.wait_ge(cx_second_split, c + 1)
                else:
                    act.wait_ge(cx_second_rest, c - NC // 2 + 1)
                layer_norm(t)

            act.wait_ge(rstd_ready, 2)
            second_norm(4)
            second_norm(5)
            exps(0)
            copy_q(1)
            second_norm(6)
            second_norm(7)
            copy_k(1)
            act.wait_ge(gate_ld, 48)
            a.activation(gate[:, :], gate_in[:, :], ACT.Tanh).then_inc(gate_ready, 1)
            z_hi(4)
            z_hi(5)
            copy_v_bank(1, 1, 0)
            z_hi(6)
            z_hi(7)
            for k in range(1, 4):
                unit(0, k, first=True)
            with act.Fori(1, PAIRS - 1) as p:
                for k in range(4):
                    unit(p, k)
            p = PAIRS - 1
            for k in range(3):
                unit(p, k, last=True)

            def norm_z(t):
                act.wait_ge(rstd_ready, 2 + t + 1)
                a.activation(acc[:, t, :], x_tok[:, t, :], ACT.Identity, bias=neg_mean[:, t:t + 1],
                             scale=rstd[:, t:t + 1]).then_inc(z_normed, 1)

            u = 4 * p + 3
            exps(u)
            norm_z(0)
            norm_z(1)
            copy_v_bank(2 * p + 1, 1, 0)
            merged_hi(3)
            copy_v_bank(2 * p + 1, 1, 1)
            norm_z(2)
            z_hi(B)
            z_hi(B + 1)
            norm_z(3)
            attended_hi(u - 1, 0)
            z_hi(B + 2)
            attended_hi(u, 1)
            z_hi(B + 3)
            norm_z(4)
            norm_z(5)
            z_hi(B + 4)
            norm_z(6)
            z_hi(B + 5)
            norm_z(7)
            z_hi(B + 6)
            z_hi(B + 7)

        @block.vector
        def _(dve):
            v = nc.vector
            step = [0]

            def link(ins):
                step[0] += 1
                ins.then_inc(vec_step, 1)
                dve.wait_ge(vec_step, step[0])

            def stats(t):
                link(v.bn_stats(bn[:, t, :], x_tok[:, t, :]))
                return v.bn_aggr(mean_var[:, t, :], bn[:, t, :])

            def z_lo(n):
                dve.wait_ge(z_hi_done, n + 1)
                o = xn_lo[:, :, tokens(n % B)]
                v.tensor_tensor(o, turned(n)[:, :].rearrange("p (c n) -> p c n", c=NC),
                                as_f32(xn_hi[:, :, tokens(n % B)]), ALU.subtract).then_inc(z_split, 1)

            def scale_x(t):
                if t == OWN:
                    dve.wait_ge(own_y_done, 1)
                else:
                    dve.wait_ge(y_done, t + (t < OWN))
                if t == 0:
                    dve.wait_ge(ln_w_in, 16)
                if t >= HB:
                    dve.wait_ge(z_turned, max(t - 1, HB))
                v.scalar_tensor_tensor(out=xs[t], in0=acc[:, t, :], scalar=rms[:, t:t + 1],
                                       in1=ln_w_b[:, :], op0=ALU.mult, op1=ALU.mult).then_inc(xs_done, 1)

            def lo(hi_done, n, out_lo, whole, hi, done):
                dve.wait_ge(hi_done, n)
                v.tensor_tensor(out_lo, whole, as_f32(hi), ALU.subtract).then_inc(done, 1)

            def lo_wqk(n, j):
                lo(wqk_hi_done[j], n, wqk_lo[:, j, :, :], wqk_stage[:, j, :, :], wqk_hi[:, j, :, :], wqk_split[j])

            def lo_wv(n):
                lo(wv_hi_done, n, wv_lo[:, :, :], wv_stage[:, :, :], wv_hi[:, :, :], wv_split)

            def lo_wo(n):
                lo(wo_hi_done, n, wo_lo[:, :, :], wo_stage[:, :, :], wo_hi[:, :, :], wo_split)

            def attended_lo(u, j):
                lo(at_hi_done, u + 1, at_lo[:, j, :], ps_pv[:, :], at_hi[:, j, :], at_split)

            def softmax_in(u, j):
                dve.wait_ge(s_done, u + 1)
                dve.wait_ge(bm_ready, u + 1)
                if not (isinstance(u, int) and u == 0):
                    dve.wait_ge(exp_done, u)
                    dve.wait_ge(p_turned, u)
                v.tensor_tensor(scores_b, ps_s[:, :].rearrange("p (b n) -> p b n", b=HB),
                                bias_mask[:, j, :, :], ALU.add).then_inc(s_biased, 1)
                dve.wait_ge(s_biased, u + 1)
                v.tensor_reduce(neg_max_t[:, :], scores_b, AX.X, ALU.max, negate=True).then_inc(neg_max, 1)

            def softmax_out(u, s):
                dve.wait_ge(exp_done, u + 1)
                v.reciprocal(row_inv[:, :], row_sum[:, :]).then_inc(row_inv_done, 1)
                dve.wait_ge(row_inv_done, u + 1)
                v.tensor_tensor(row_inv[:, :], row_inv[:, :], row_used[:, s * HB:(s + 1) * HB], ALU.mult).then_inc(row_scale, 1)
                dve.wait_ge(row_scale, u + 1)
                v.tensor_tensor(scores[:, :].rearrange("p (j b r) -> p b j r", j=NSQ, b=HB),
                                prob[:, :].rearrange("p (b j r) -> p b j r", j=NSQ, b=HB),
                                row_inv[:, :].unsqueeze(2).unsqueeze(3).to_broadcast([P, HB, NSQ, SQ]),
                                ALU.mult).then_inc(p_norm, 1)
                dve.wait_ge(p_norm, u + 1)
                v.transpose(prob[:, :], scores[:, :]).then_inc(p_turned, 1)

            def add_out(done, s, b):
                dve.wait_ge(o_done, done + 1)
                t = s * HB + b
                v.tensor_tensor(acc[:, t, :], ps_x[b % 2][:, :], acc[:, t, :], ALU.add).then_inc(o_added, 1)

            def unit(p, k, first=False, last=False):
                u, s, j = 4 * p + k, k // 2, k % 2
                out_from = None if k % 2 == 0 else 8 * p - 6 + 2 * k
                softmax_in(u, j)
                if k % 2 == 0:
                    attended_lo(u - 2, 0)
                if out_from is not None:
                    add_out(out_from, 1 - s, 0)
                softmax_out(u, s)
                if out_from is not None:
                    add_out(out_from + 1, 1 - s, 1)
                if k == 2:
                    lo_wo(p + 1)
                    if not last:
                        lo_wqk(p + 2, 0)
                if k == 3:
                    lo_wqk(p + 2, 1)
                    lo_wv(p + 2)
                if out_from is not None:
                    add_out(out_from + 2, 1 - s, 2)
                    add_out(out_from + 3, 1 - s, 3)
                if k % 2 == 0:
                    attended_lo(u - 1, 1)
                if last and k == 0:
                    merged(0)
                    for t in range(HB):
                        gate_x(t)
                if last and k < 2:
                    merged(k + 1)

            def gate_x(t):
                if t == 0:
                    dve.wait_ge(gate_ready, 1)
                dve.wait_ge(o_added, 8 * PAIRS - 12 + t // HB * HB)
                v.scalar_tensor_tensor(out=x_tok[:, t, :], in0=acc[:, t, :], scalar=gate[:, 0:1],
                                       in1=x_tok[:, t, :], op0=ALU.mult, op1=ALU.add).then_inc(x_gated, 1)

            def merged(c):
                if c == 0:
                    dve.wait_ge(wf_in, 16)
                dve.wait_ge(m_done, c + 1)
                v.tensor_tensor(wf[:, c, :], ps_z[:, :], wf[:, c, :], ALU.add).then_inc(m_added, 1)
                lo(m_hi_done, c + 1, wf_lo[:, c, :], wf[:, c, :], wf_hi[:, c, :], m_split)

            def lo_cx(c):
                lo(cx_hi_done, c + 1, cx_lo[:, c, half(0)], ctx_stage[0][:, c, :], cx_hi[:, c, half(0)], cx_first_split)

            def tile_stats(t):
                dve.wait_ge(x_in[t], 16)
                link(stats(t))

            def half_stats(s):
                h = slice(s * HB, (s + 1) * HB)
                link(v.tensor_scalar(ve[:, h], mean_var[:, h, 1], EPS, None, ALU.add))
                link(v.reciprocal(ve_inv[:, h], ve[:, h]))
                link(v.tensor_tensor(ve_inv[:, h], ve_inv[:, h], mean_var[:, h, 1], ALU.mult))
                v.tensor_scalar(rms_in[:, h], ve_inv[:, h], EPS, None, ALU.add).then_inc(norm_in_ready, 1)

            def neg_means(s):
                h = slice(s * HB, (s + 1) * HB)
                dve.wait_ge(norm_out_ready, s + 1)
                v.scalar_tensor_tensor(out=neg_mean[:, h], in0=mean_var[:, h, 0], scalar=-1.0,
                                       in1=rstd[:, h], op0=ALU.mult, op1=ALU.mult).then_inc(rstd_ready, 1)

            lo_cx(0)
            lo(first_k_hi, 1, wqk_lo[:, 0, 1, :], wqk_stage[:, 0, 1, :], wqk_hi[:, 0, 1, :], first_k_split)
            for c in range(1, NC):
                lo_cx(c)
            lo(wv_hi_done, 1, wv_lo[:, :NC // 2, :], wv_stage[:, :NC // 2, :], wv_hi[:, :NC // 2, :], wv_split)
            for t in range(HB):
                tile_stats(t)
            half_stats(0)
            lo_wqk(1, 1)
            tile_stats(4)
            neg_means(0)
            tile_stats(5)
            for t in range(HB):
                scale_x(t)
            for t in range(HB):
                z_lo(t)
            tile_stats(6)
            tile_stats(7)
            half_stats(1)
            for c in range(NC // 2, NC):
                lo(cx_hi_done, NC + c + 1, cx_lo[:, c, half(1)], ctx_stage[1][:, c, :], cx_hi[:, c, half(1)], cx_second_rest)

            def rows_used():
                dve.wait_ge(mask_ready, 1)
                link(v.tensor_reduce(row_best[:, :], mask_add[:, :, :], AX.X, ALU.max))
                v.tensor_scalar(row_used[:, :], row_best[:, :], -0.5 * MASKED, None, ALU.is_ge).then_inc(used_ready, 1)
                dve.wait_ge(used_ready, 1)

            neg_means(1)
            softmax_in(0, 0)
            rows_used()
            scale_x(4)
            scale_x(5)
            softmax_out(0, 0)
            z_lo(4)
            scale_x(6)
            z_lo(5)
            scale_x(7)
            softmax_in(1, 1)
            z_lo(6)
            z_lo(7)
            softmax_out(1, 0)
            for k in range(2, 4):
                unit(0, k, first=True)
            with dve.Fori(1, PAIRS - 1) as p:
                for k in range(4):
                    unit(p, k)
            p = PAIRS - 1
            for k in range(3):
                unit(p, k, last=True)

            def gate_out(t):
                dve.wait_ge(x_gated, t + 1)
                dve.wait_ge(o_done, 8 * PAIRS - 8 + t + 1)
                v.scalar_tensor_tensor(out=x_tok[:, t, :], in0=ps_x[t % 2][:, :], scalar=gate[:, 0:1],
                                       in1=x_tok[:, t, :], op0=ALU.mult, op1=ALU.add).then_inc(o_added, 1)

            def x2_stats(t):
                dve.wait_ge(o_added, 8 * PAIRS - 8 + t + 1)
                stats(t).then_inc(x2_done, 1)

            def result(t):
                dve.wait_ge(f_done, t + 1)
                dve.wait_ge(x2_biased, t + 1)
                v.scalar_tensor_tensor(out=acc[:, t, :], in0=ps_f[t % 2][:, :], scalar=gate[:, 1:2],
                                       in1=x_tok[:, t, :], op0=ALU.mult, op1=ALU.add).then_inc(f_out, 1)

            u = 4 * p + 3
            softmax_in(u, 1)
            gate_out(0)
            gate_out(1)
            gate_out(2)
            softmax_out(u, 1)
            x2_stats(0)
            gate_out(3)
            for t in range(1, HB):
                x2_stats(t)
            merged(3)
            z_lo(B)
            z_lo(B + 1)
            attended_lo(u - 1, 0)
            for t in range(HB, B):
                gate_x(t)
            z_lo(B + 2)
            result(0)
            attended_lo(u, 1)
            z_lo(B + 3)
            gate_out(4)
            x2_stats(4)
            result(1)
            for t in range(5, B):
                gate_out(t)
                x2_stats(t)
            for t in range(4, B):
                z_lo(B + t)
                result(t - 2)
            result(B - 2)
            result(B - 1)


def kernel(x, ctx_4096, mask_BxSxS2_bk0, g_xattn, g_ffn, L0_xattn_position_bias, L0_xattn_ln_weight,
           L0_xattn_w_q, L0_xattn_w_k, L0_xattn_w_v, L0_xattn_w_out, L0_ffn_lora_A, L0_ffn_lora_B,
           L0_ffn_W, L0_ffn_bias, L0_ffn_lora_weights):
    import numpy as np
    import concourse.bacc as bacc
    from concourse.bass_utils import run_bass_kernel_spmd

    def laid(a, shape, axes, to):
        return np.ascontiguousarray(np.asarray(a).reshape(shape).transpose(axes).reshape(to))

    arrays = {
        "x": np.ascontiguousarray(x),
        "ctx_t": laid(ctx_4096, (2, HT, NC, P), (0, 3, 2, 1), (2, P, NC, HT)),
        "mask": np.ascontiguousarray(np.asarray(mask_BxSxS2_bk0).transpose(1, 0, 2)),
        "g_xattn": np.ascontiguousarray(g_xattn),
        "g_ffn": np.ascontiguousarray(g_ffn),
        "bias": laid(L0_xattn_position_bias, (PAIRS, 2, S, S), (0, 2, 1, 3), (PAIRS, S, 2, S)),
        "ln_w": np.ascontiguousarray(L0_xattn_ln_weight),
        "wq": laid(L0_xattn_w_q, (H, DH, NC, P), (0, 3, 2, 1), (H, P, NC * DH)),
        "wk": laid(L0_xattn_w_k, (H, DH, NC, P), (0, 3, 2, 1), (H, P, NC * DH)),
        "wv": laid(L0_xattn_w_v, (PAIRS, 2 * DH, NC, P), (0, 3, 2, 1), (PAIRS, P, NC, 2 * DH)),
        "wo": laid(L0_xattn_w_out, (D, PAIRS, 2, DH), (1, 3, 2, 0), (PAIRS, DH, 2, D)),
        "lora_a": laid(L0_ffn_lora_A, (N_LORA * RANK, D), (0, 1), (N_LORA * RANK, D)),
        "lora_bt": laid(L0_ffn_lora_B, (N_LORA, D, RANK), (0, 2, 1), (N_LORA * RANK, D)),
        "w_t": laid(L0_ffn_W, (D, NC, P), (2, 1, 0), (P, NC, D)),
        "ffn_bias": np.ascontiguousarray(L0_ffn_bias),
        "lora_w": np.repeat(np.asarray(L0_ffn_lora_weights), RANK).reshape(P, 1),
    }
    nc = bacc.Bacc("TRN2", target_bir_lowering=False, num_devices=1)
    args = [nc.dram_tensor(f"{name}_dram", a.shape, mybir.dt.from_np(a.dtype), kind="ExternalInput").ap()
            for name, a in arrays.items()]
    out = nc.dram_tensor("out_dram", (B, S, D), FP32, kind="ExternalOutput").ap()
    gated_block(nc, *args, out)
    r = run_bass_kernel_spmd(nc, [{f"{name}_dram": a for name, a in arrays.items()}], core_ids=[0])
    return r.results[0]["out_dram"]
```
